# Optimizing a Trainium2 kernel written in Bass

```python
import numpy as np
import jax
import jax.numpy as jnp

def _softmax(x, axis=-1):
    return jax.nn.softmax(x, axis=axis)

def _gelu(x):
    return jax.nn.gelu(x, approximate=True)

def _silu(x):
    return jax.nn.silu(x)

def _sigmoid(x):
    return jax.nn.sigmoid(x)

def _layernorm(x, axis=-1, eps=1e-05):
    m = jnp.mean(x, axis=axis, keepdims=True)
    v = jnp.var(x, axis=axis, keepdims=True)
    return (x - m) / jnp.sqrt(v + eps)

def _scatter_add(tgt, idx, src, axis=0):
    return tgt.at[idx].add(src)

def _segment_sum(src, seg, n):
    return jax.ops.segment_sum(src, seg, n)
kernel_name = 'mk_recurrent_d1_jaxref_r8_299189'

def setup_inputs(seed: int=0):
    np.random.seed(seed)
    _w = jnp.asarray

    def _L0_attn_setup():
        import jax, jax.numpy as jnp
        import numpy as np
        from jax import lax
        D_MODEL = 128
        D_STATE = 16
        D_CONV = 4
        EXPAND = 2
        D_INNER = EXPAND * D_MODEL
        DT_RANK = D_MODEL // 16
        BATCH = 2
        SEQLEN = 128

        def silu(v):
            return v * jax.nn.sigmoid(v)

        def _mamba_forward(hidden_states, in_proj_w, in_proj_b, conv_w, conv_b, x_proj_w, dt_proj_w, dt_proj_b, A_log, D_param, out_proj_w, out_proj_b):
            b, l, _ = hidden_states.shape
            d_inner, d_state = A_log.shape
            d_conv = conv_w.shape[-1]
            xz = hidden_states @ in_proj_w.T + in_proj_b
            x, z = jnp.split(xz, 2, axis=-1)
            x_ch = x.transpose(0, 2, 1)
            x_conv = lax.conv_general_dilated(x_ch, conv_w[:, None, :], window_strides=(1,), padding=[(d_conv - 1, 0)], feature_group_count=d_inner, dimension_numbers=('NCH', 'OIH', 'NCH'))
            x = silu((x_conv + conv_b[None, :, None]).transpose(0, 2, 1))
            x_dbl = x @ x_proj_w.T
            dt_rank = x_proj_w.shape[0] - 2 * d_state
            dt_lr, Bm, Cm = jnp.split(x_dbl, [dt_rank, dt_rank + d_state], axis=-1)
            dt = jax.nn.softplus(dt_lr @ dt_proj_w.T + dt_proj_b)
            A = -jnp.exp(A_log)
            deltaA = jnp.exp(dt[..., None] * A)
            deltaBu = (dt * x)[..., None] * Bm[:, :, None, :]

            def step(h, inp):
                dA_t, dBu_t, C_t = inp
                h = dA_t * h + dBu_t
                y_t = jnp.einsum('bdn,bn->bd', h, C_t)
                return (h, y_t)
            h0 = jnp.zeros((b, d_inner, d_state), dtype=x.dtype)
            _, ys = lax.scan(step, h0, (deltaA.transpose(1, 0, 2, 3), deltaBu.transpose(1, 0, 2, 3), Cm.transpose(1, 0, 2)))
            y = ys.transpose(1, 0, 2) + x * D_param
            y = y * silu(z)
            return y @ out_proj_w.T + out_proj_b
        key = jax.random.key(seed)
        ks = jax.random.split(key, 8)
        g = lambda k, shp, sc: jax.random.normal(k, shp, dtype=jnp.float32) * sc
        hidden_states = g(ks[0], (BATCH, SEQLEN, D_MODEL), 1.0)
        in_proj_w = g(ks[1], (2 * D_INNER, D_MODEL), D_MODEL ** (-0.5))
        in_proj_b = jnp.zeros((2 * D_INNER,), jnp.float32)
        conv_w = g(ks[2], (D_INNER, D_CONV), D_CONV ** (-0.5))
        conv_b = jnp.zeros((D_INNER,), jnp.float32)
        x_proj_w = g(ks[3], (DT_RANK + 2 * D_STATE, D_INNER), D_INNER ** (-0.5))
        dt_std = DT_RANK ** (-0.5)
        dt_proj_w = jax.random.uniform(ks[4], (D_INNER, DT_RANK), jnp.float32, -dt_std, dt_std)
        dt = jnp.exp(jax.random.uniform(ks[5], (D_INNER,), jnp.float32) * (np.log(0.1) - np.log(0.001)) + np.log(0.001))
        dt = jnp.clip(dt, 0.0001)
        dt_proj_b = dt + jnp.log(-jnp.expm1(-dt))
        A_log = jnp.log(jnp.broadcast_to(jnp.arange(1, D_STATE + 1, dtype=jnp.float32), (D_INNER, D_STATE)))
        D_param = jnp.ones((D_INNER,), jnp.float32)
        out_proj_w = g(ks[6], (D_MODEL, D_INNER), D_INNER ** (-0.5))
        out_proj_b = jnp.zeros((D_MODEL,), jnp.float32)
        return dict(hidden_states=hidden_states, in_proj_w=in_proj_w, in_proj_b=in_proj_b, conv_w=conv_w, conv_b=conv_b, x_proj_w=x_proj_w, dt_proj_w=dt_proj_w, dt_proj_b=dt_proj_b, A_log=A_log, D_param=D_param, out_proj_w=out_proj_w, out_proj_b=out_proj_b)
    _L0_attn_in = _L0_attn_setup()

    def _L0_ffn_setup():
        import jax, jax.numpy as jnp
        import numpy as np
        DIM = 128
        DEPTH = 6
        HEADS = 16
        DIM_HEAD = 64
        WINDOW = 32
        INNER = HEADS * DIM_HEAD
        DIM_INNER = int(DIM * 4 * 2 / 3)
        QK_SCALE = 8.0

        def shift_tokens(t):
            a, s = jnp.split(t, 2, -1)
            s = jnp.pad(s, ((0, 0), (1, 0), (0, 0)))[:, :-1]
            return jnp.concatenate([a, s], -1)

        def l2norm(t):
            return t / jnp.maximum(jnp.linalg.norm(t, axis=-1, keepdims=True), 1e-12)

        def rotate_half(x):
            x1, x2 = jnp.split(x, 2, -1)
            return jnp.concatenate([-x2, x1], -1)

        def rotary_tables(n):
            half = jnp.arange(0, DIM_HEAD, 2, dtype=jnp.float32)
            inv_freq = 1.0 / 10000.0 ** (half / DIM_HEAD)
            t = jnp.arange(n, dtype=jnp.float32)
            freqs = t[:, None] * inv_freq[None, :]
            freqs = jnp.concatenate([freqs, freqs], -1)
            base_scale = (half + 0.4 * DIM_HEAD) / (1.4 * DIM_HEAD)
            power = (t - n // 2) / (WINDOW // 2)
            scale = base_scale[None, :] ** power[:, None]
            scale = jnp.concatenate([scale, scale], -1)
            return (freqs, scale)

        def local_attention(q, k, v):
            b, h, n, d = q.shape
            w = WINDOW
            nw = n // w
            bq = q.reshape(b, h, nw, w, d)
            bk = k.reshape(b, h, nw, w, d)
            bv = v.reshape(b, h, nw, w, d)

            def look(t):
                p = jnp.pad(t, ((0, 0), (0, 0), (1, 0), (0, 0), (0, 0)))
                return jnp.concatenate([p[:, :, :nw], p[:, :, 1:]], axis=3)
            bk2, bv2 = (look(bk), look(bv))
            seq = jnp.arange(n).reshape(nw, w)
            seq_p = jnp.pad(seq, ((1, 0), (0, 0)), constant_values=-1)
            jt = jnp.concatenate([seq_p[:nw], seq_p[1:]], axis=1)
            it = seq[:, :, None]
            jb = jt[:, None, :]
            mask = (it < jb) | (it > jb + w) | (jb == -1)
            sim = jnp.einsum('bhwie,bhwje->bhwij', bq, bk2) * QK_SCALE
            sim = jnp.where(mask, -jnp.finfo(sim.dtype).max, sim)
            attn = jax.nn.softmax(sim, -1)
            out = jnp.einsum('bhwij,bhwje->bhwie', attn, bv2)
            return out.reshape(b, h, n, d)

        def attn_layer(x, Wqkv, qs, ksc, Wo):
            b, n, _ = x.shape
            qkv = x @ Wqkv
            q, k, v = jnp.split(qkv, 3, -1)
            sh = lambda t: t.reshape(b, n, HEADS, DIM_HEAD).transpose(0, 2, 1, 3)
            q, k, v = (sh(q), sh(k), sh(v))
            q = l2norm(q) * qs
            k = l2norm(k) * ksc
            freqs, scale = rotary_tables(n)
            cos, sin = (jnp.cos(freqs), jnp.sin(freqs))
            q = q * cos * scale + rotate_half(q) * sin * scale
            inv = 1.0 / scale
            k = k * cos * inv + rotate_half(k) * sin * inv
            out = local_attention(q, k, v)
            out = out.transpose(0, 2, 1, 3).reshape(b, n, INNER)
            return out @ Wo

        def ffn_layer(x, g, bln, W1, b1, W2, b2):
            mu = x.mean(-1, keepdims=True)
            var = ((x - mu) ** 2).mean(-1, keepdims=True)
            xn = (x - mu) / jnp.sqrt(var + 1e-05) * g + bln
            hg = xn @ W1 + b1
            a, gate = jnp.split(hg, 2, -1)
            return a * jax.nn.gelu(gate, approximate=False) @ W2 + b2
        key = jax.random.key(seed)
        ks = jax.random.split(key, 8)
        B, N = (2, 256)
        init = lambda k, shape: jax.random.normal(k, shape, jnp.float32) * 0.02
        return {'x': jax.random.normal(ks[0], (B, N, DIM), jnp.float32), 'Wqkv': init(ks[1], (DEPTH, DIM, 3 * INNER)), 'q_scale': jnp.ones((DEPTH, DIM_HEAD), jnp.float32), 'k_scale': jnp.ones((DEPTH, DIM_HEAD), jnp.float32), 'Wo': init(ks[2], (DEPTH, INNER, DIM)), 'ln_g': jnp.ones((DEPTH, DIM), jnp.float32), 'ln_b': jnp.zeros((DEPTH, DIM), jnp.float32), 'W1': init(ks[3], (DEPTH, DIM, 2 * DIM_INNER)), 'b1': jnp.zeros((DEPTH, 2 * DIM_INNER), jnp.float32), 'W2': init(ks[4], (DEPTH, DIM_INNER, DIM)), 'b2': jnp.zeros((DEPTH, DIM), jnp.float32)}
    _L0_ffn_in = _L0_ffn_setup()
    _d = {'L0_attn_hidden_states': _L0_attn_in['hidden_states'], 'L0_attn_in_proj_w': _L0_attn_in['in_proj_w'], 'L0_attn_in_proj_b': _L0_attn_in['in_proj_b'], 'L0_attn_conv_w': _L0_attn_in['conv_w'], 'L0_attn_conv_b': _L0_attn_in['conv_b'], 'L0_attn_x_proj_w': _L0_attn_in['x_proj_w'], 'L0_attn_dt_proj_w': _L0_attn_in['dt_proj_w'], 'L0_attn_dt_proj_b': _L0_attn_in['dt_proj_b'], 'L0_attn_A_log': _L0_attn_in['A_log'], 'L0_attn_D_param': _L0_attn_in['D_param'], 'L0_attn_out_proj_w': _L0_attn_in['out_proj_w'], 'L0_attn_out_proj_b': _L0_attn_in['out_proj_b'], 'L0_ffn_Wqkv': _L0_ffn_in['Wqkv'], 'L0_ffn_q_scale': _L0_ffn_in['q_scale'], 'L0_ffn_k_scale': _L0_ffn_in['k_scale'], 'L0_ffn_Wo': _L0_ffn_in['Wo'], 'L0_ffn_ln_g': _L0_ffn_in['ln_g'], 'L0_ffn_ln_b': _L0_ffn_in['ln_b'], 'L0_ffn_W1': _L0_ffn_in['W1'], 'L0_ffn_b1': _L0_ffn_in['b1'], 'L0_ffn_W2': _L0_ffn_in['W2'], 'L0_ffn_b2': _L0_ffn_in['b2']}
    _x0 = _d['L0_attn_hidden_states']
    _d['L0_attn_hidden_states'] = jax.random.normal(jax.random.fold_in(jax.random.key(seed), 1), (2, 2048, 128), dtype=_x0.dtype)
    del _x0
    return _d

def reference(L0_attn_hidden_states, L0_attn_in_proj_w, L0_attn_in_proj_b, L0_attn_conv_w, L0_attn_conv_b, L0_attn_x_proj_w, L0_attn_dt_proj_w, L0_attn_dt_proj_b, L0_attn_A_log, L0_attn_D_param, L0_attn_out_proj_w, L0_attn_out_proj_b, L0_ffn_Wqkv, L0_ffn_q_scale, L0_ffn_k_scale, L0_ffn_Wo, L0_ffn_ln_g, L0_ffn_ln_b, L0_ffn_W1, L0_ffn_b1, L0_ffn_W2, L0_ffn_b2):

    def _L0_attn_ref(hidden_states, in_proj_w, in_proj_b, conv_w, conv_b, x_proj_w, dt_proj_w, dt_proj_b, A_log, D_param, out_proj_w, out_proj_b):
        import jax, jax.numpy as jnp
        import numpy as np
        from jax import lax
        D_MODEL = 128
        D_STATE = 16
        D_CONV = 4
        EXPAND = 2
        D_INNER = EXPAND * D_MODEL
        DT_RANK = D_MODEL // 16
        BATCH = 2
        SEQLEN = 128

        def silu(v):
            return v * jax.nn.sigmoid(v)

        def _mamba_forward(hidden_states, in_proj_w, in_proj_b, conv_w, conv_b, x_proj_w, dt_proj_w, dt_proj_b, A_log, D_param, out_proj_w, out_proj_b):
            b, l, _ = hidden_states.shape
            d_inner, d_state = A_log.shape
            d_conv = conv_w.shape[-1]
            xz = hidden_states @ in_proj_w.T + in_proj_b
            x, z = jnp.split(xz, 2, axis=-1)
            x_ch = x.transpose(0, 2, 1)
            x_conv = lax.conv_general_dilated(x_ch, conv_w[:, None, :], window_strides=(1,), padding=[(d_conv - 1, 0)], feature_group_count=d_inner, dimension_numbers=('NCH', 'OIH', 'NCH'))
            x = silu((x_conv + conv_b[None, :, None]).transpose(0, 2, 1))
            x_dbl = x @ x_proj_w.T
            dt_rank = x_proj_w.shape[0] - 2 * d_state
            dt_lr, Bm, Cm = jnp.split(x_dbl, [dt_rank, dt_rank + d_state], axis=-1)
            dt = jax.nn.softplus(dt_lr @ dt_proj_w.T + dt_proj_b)
            A = -jnp.exp(A_log)
            deltaA = jnp.exp(dt[..., None] * A)
            deltaBu = (dt * x)[..., None] * Bm[:, :, None, :]

            def step(h, inp):
                dA_t, dBu_t, C_t = inp
                h = dA_t * h + dBu_t
                y_t = jnp.einsum('bdn,bn->bd', h, C_t)
                return (h, y_t)
            h0 = jnp.zeros((b, d_inner, d_state), dtype=x.dtype)
            _, ys = lax.scan(step, h0, (deltaA.transpose(1, 0, 2, 3), deltaBu.transpose(1, 0, 2, 3), Cm.transpose(1, 0, 2)))
            y = ys.transpose(1, 0, 2) + x * D_param
            y = y * silu(z)
            return y @ out_proj_w.T + out_proj_b
        return _mamba_forward(hidden_states, in_proj_w, in_proj_b, conv_w, conv_b, x_proj_w, dt_proj_w, dt_proj_b, A_log, D_param, out_proj_w, out_proj_b)

    def _L0_ffn_ref(x, Wqkv, q_scale, k_scale, Wo, ln_g, ln_b, W1, b1, W2, b2):
        import jax, jax.numpy as jnp
        import numpy as np
        DIM = 128
        DEPTH = 6
        HEADS = 16
        DIM_HEAD = 64
        WINDOW = 32
        INNER = HEADS * DIM_HEAD
        DIM_INNER = int(DIM * 4 * 2 / 3)
        QK_SCALE = 8.0

        def shift_tokens(t):
            a, s = jnp.split(t, 2, -1)
            s = jnp.pad(s, ((0, 0), (1, 0), (0, 0)))[:, :-1]
            return jnp.concatenate([a, s], -1)

        def l2norm(t):
            return t / jnp.maximum(jnp.linalg.norm(t, axis=-1, keepdims=True), 1e-12)

        def rotate_half(x):
            x1, x2 = jnp.split(x, 2, -1)
            return jnp.concatenate([-x2, x1], -1)

        def rotary_tables(n):
            half = jnp.arange(0, DIM_HEAD, 2, dtype=jnp.float32)
            inv_freq = 1.0 / 10000.0 ** (half / DIM_HEAD)
            t = jnp.arange(n, dtype=jnp.float32)
            freqs = t[:, None] * inv_freq[None, :]
            freqs = jnp.concatenate([freqs, freqs], -1)
            base_scale = (half + 0.4 * DIM_HEAD) / (1.4 * DIM_HEAD)
            power = (t - n // 2) / (WINDOW // 2)
            scale = base_scale[None, :] ** power[:, None]
            scale = jnp.concatenate([scale, scale], -1)
            return (freqs, scale)

        def local_attention(q, k, v):
            b, h, n, d = q.shape
            w = WINDOW
            nw = n // w
            bq = q.reshape(b, h, nw, w, d)
            bk = k.reshape(b, h, nw, w, d)
            bv = v.reshape(b, h, nw, w, d)

            def look(t):
                p = jnp.pad(t, ((0, 0), (0, 0), (1, 0), (0, 0), (0, 0)))
                return jnp.concatenate([p[:, :, :nw], p[:, :, 1:]], axis=3)
            bk2, bv2 = (look(bk), look(bv))
            seq = jnp.arange(n).reshape(nw, w)
            seq_p = jnp.pad(seq, ((1, 0), (0, 0)), constant_values=-1)
            jt = jnp.concatenate([seq_p[:nw], seq_p[1:]], axis=1)
            it = seq[:, :, None]
            jb = jt[:, None, :]
            mask = (it < jb) | (it > jb + w) | (jb == -1)
            sim = jnp.einsum('bhwie,bhwje->bhwij', bq, bk2) * QK_SCALE
            sim = jnp.where(mask, -jnp.finfo(sim.dtype).max, sim)
            attn = jax.nn.softmax(sim, -1)
            out = jnp.einsum('bhwij,bhwje->bhwie', attn, bv2)
            return out.reshape(b, h, n, d)

        def attn_layer(x, Wqkv, qs, ksc, Wo):
            b, n, _ = x.shape
            qkv = x @ Wqkv
            q, k, v = jnp.split(qkv, 3, -1)
            sh = lambda t: t.reshape(b, n, HEADS, DIM_HEAD).transpose(0, 2, 1, 3)
            q, k, v = (sh(q), sh(k), sh(v))
            q = l2norm(q) * qs
            k = l2norm(k) * ksc
            freqs, scale = rotary_tables(n)
            cos, sin = (jnp.cos(freqs), jnp.sin(freqs))
            q = q * cos * scale + rotate_half(q) * sin * scale
            inv = 1.0 / scale
            k = k * cos * inv + rotate_half(k) * sin * inv
            out = local_attention(q, k, v)
            out = out.transpose(0, 2, 1, 3).reshape(b, n, INNER)
            return out @ Wo

        def ffn_layer(x, g, bln, W1, b1, W2, b2):
            mu = x.mean(-1, keepdims=True)
            var = ((x - mu) ** 2).mean(-1, keepdims=True)
            xn = (x - mu) / jnp.sqrt(var + 1e-05) * g + bln
            hg = xn @ W1 + b1
            a, gate = jnp.split(hg, 2, -1)
            return a * jax.nn.gelu(gate, approximate=False) @ W2 + b2
        for i in range(DEPTH):
            x = attn_layer(shift_tokens(x), Wqkv[i], q_scale[i], k_scale[i], Wo[i]) + x
            x = ffn_layer(shift_tokens(x), ln_g[i], ln_b[i], W1[i], b1[i], W2[i], b2[i]) + x
        return x
    x = L0_attn_hidden_states
    xn = _layernorm(x, axis=-1)
    s = _L0_attn_ref(xn, L0_attn_in_proj_w, L0_attn_in_proj_b, L0_attn_conv_w, L0_attn_conv_b, L0_attn_x_proj_w, L0_attn_dt_proj_w, L0_attn_dt_proj_b, L0_attn_A_log, L0_attn_D_param, L0_attn_out_proj_w, L0_attn_out_proj_b)
    g = _silu(_L0_ffn_ref(xn, L0_ffn_Wqkv, L0_ffn_q_scale, L0_ffn_k_scale, L0_ffn_Wo, L0_ffn_ln_g, L0_ffn_ln_b, L0_ffn_W1, L0_ffn_b1, L0_ffn_W2, L0_ffn_b2))
    x = x + s * g
    return x

_drawn_inputs = setup_inputs


def setup_inputs(seed=0):
    import zlib

    import numpy as np

    out = dict(_drawn_inputs(seed))
    spreads = {'L0_attn_in_proj_b': (0.0, 0.1),
     'L0_attn_conv_b': (0.0, 0.308),
     'L0_attn_D_param': (1.0, 0.2),
     'L0_attn_out_proj_b': (0.0, 0.1),
     'L0_ffn_q_scale': (1.0, 0.6),
     'L0_ffn_k_scale': (1.0, 0.6),
     'L0_ffn_ln_g': (1.0, 0.6),
     'L0_ffn_ln_b': (0.0, 0.8),
     'L0_ffn_b1': (0.0, 0.8),
     'L0_ffn_b2': (0.0, 0.537)}
    factors = {'L0_attn_dt_proj_w': 5.069,
     'L0_attn_dt_proj_b': 3.171,
     'L0_ffn_W1': 6.86,
     'L0_ffn_W2': 6.729}
    for name, (base, spread) in spreads.items():
        noise = np.random.default_rng([zlib.crc32(name.encode()), seed]).standard_normal(out[name].shape)
        drawn = base * np.exp(spread * noise) if base else spread * noise
        out[name] = jnp.asarray(drawn.astype(out[name].dtype))
    for name, factor in factors.items():
        out[name] = (out[name] * factor).astype(out[name].dtype)
    return out
```

```python
from contextlib import ExitStack

import numpy as np

import concourse.bass as bass
from concourse import mybir

F32 = mybir.dt.float32
BF16 = mybir.dt.bfloat16
ALU = mybir.AluOpType
ACT = mybir.ActivationFunctionType
AX_X = mybir.AxisListType.X

P = 128
BATCH, SEQ, DIM = 2, 2048, 128
TOKENS = BATCH * SEQ
NTOK = TOKENS // P
INNER_M = 256
STATE = 16
DT_RANK = 8
CONV = 4
CH = 512
NCH = SEQ // CH
DEPTH, HEADS, DH, WIN = 6, 16, 64, 32
INNER = HEADS * DH
FF = 341
FFR = FF - 2 * P
TILE = 256
NT = SEQ // TILE
NWIN = TILE // WIN
HALO = WIN
PAD = 64
ROW = PAD + SEQ
UNITS = 4
TAB = 4 * TILE + 1
QK_SCALE = 8.0
EPS = 1e-5
NORM_FLOOR = 1e-12
LN_SHIFT = 20
MASKED = -1e24
QA, QB, KA, KB, LG, LB, B2, B1A, B1G = 0, 1, 2, 3, 4, 5, 6, 7, 10
NPAR = 13


def wait_alone(eng, sem, value, spare):
    eng.wait_ge(sem, value)
    eng.sem_inc(spare, 1)


def pos(w):
    return (w % 2) * 4 + w // 2


def phase_norm(nc, x, xt, identity):
    with ExitStack() as ctx:
        def sb(name, shape, dt=F32):
            return ctx.enter_context(nc.sbuf_tensor(name, shape, dt))

        def sem(name):
            return ctx.enter_context(nc.semaphore(name))

        xin = sb("ln_x", [P, NTOK, DIM])
        sq = sb("ln_sq", [P, NTOK, DIM])
        mean = sb("ln_mean", [P, NTOK])
        var = sb("ln_var", [P, NTOK])
        dev = sb("ln_dev", [P, NTOK])
        rstd = sb("ln_rstd", [P, NTOK])
        ps = [ctx.enter_context(nc.psum_tensor(f"ln_ps{i}", [P, 512], F32)) for i in range(2)]
        ident = sb("ln_ident", [P, P])
        loaded, zeroed, step, squared, rooted = (sem(n) for n in ("ln_loaded", "ln_zeroed", "ln_step", "ln_squared", "ln_rooted"))
        turned, copied = sem("ln_turned"), sem("ln_copied")
        groups = TOKENS // 512
        block = ctx.enter_context(nc.Block())

        @block.sync
        def _(sp):
            sp.dma_start(xin[:], x.rearrange("b (n p) d -> p (b n) d", p=P)).then_inc(loaded, 16)
            sp.dma_start(ident[:], identity).then_inc(loaded, 16)

        @block.gpsimd
        def _(pool):
            for b in range(2 * BATCH):
                nc.gpsimd.memset(xt[:, b * ROW:b * ROW + PAD], 0.0).then_inc(zeroed, 1)
            pool.wait_ge(zeroed, 2 * BATCH)

        @block.scalar
        def _(act):
            act.wait_ge(step, 2)
            nc.scalar.activation(sq[:], xin[:], ACT.Square).then_inc(squared, 1)
            act.wait_ge(step, 4)
            nc.scalar.activation(dev[:], var[:], ACT.Sqrt).then_inc(rooted, 1)

        @block.vector
        def _(dve):
            def bc(t):
                return t[:].unsqueeze(2).broadcast_to([P, NTOK, DIM])
            dve.wait_ge(loaded, 32)
            nc.vector.tensor_reduce(mean[:], xin[:], AX_X, ALU.add).then_inc(step, 1)
            dve.wait_ge(step, 1)
            nc.vector.tensor_scalar(rstd[:], mean[:], 1.0 / DIM, None, ALU.mult).then_inc(rooted, 1)
            dve.wait_ge(rooted, 1)
            nc.vector.tensor_tensor(xin[:], xin[:], bc(rstd), ALU.subtract).then_inc(step, 1)
            dve.wait_ge(squared, 1)
            nc.vector.tensor_reduce(mean[:], sq[:], AX_X, ALU.add).then_inc(step, 1)
            dve.wait_ge(step, 3)
            nc.vector.tensor_scalar(var[:], mean[:], 1.0 / DIM, EPS, ALU.mult, ALU.add).then_inc(step, 1)
            dve.wait_ge(rooted, 2)
            nc.vector.reciprocal(rstd[:], dev[:]).then_inc(step, 1)
            dve.wait_ge(step, 5)
            nc.vector.tensor_tensor(xin[:], xin[:], bc(rstd), ALU.mult).then_inc(step, 1)
            for g in range(groups):
                dve.wait_ge(turned, g + 1)
                b, c = divmod(g, SEQ // 512)
                at = b * ROW + PAD + 512 * c
                nc.vector.tensor_copy(xt[:, at:at + 512], ps[g % 2][:]).then_inc(copied, 1)

        @block.tensor
        def _(pe):
            pe.wait_ge(step, 6)
            for g in range(groups):
                if g >= 2:
                    pe.wait_ge(copied, g - 1)
                for k in range(4):
                    last = nc.tensor.transpose(ps[g % 2][:, P * k:P * (k + 1)], xin[:, 4 * g + k, :], ident[:])
                last.then_inc(turned, 1)


def phase_mamba(nc, xt, d, s_dram):
    H2 = INNER_M // P
    with ExitStack() as ctx:
        def sb(name, shape, dt=F32):
            return ctx.enter_context(nc.sbuf_tensor(name, shape, dt))

        def psum(name, shape):
            return ctx.enter_context(nc.psum_tensor(name, shape, F32))

        def sem(name):
            return ctx.enter_context(nc.semaphore(name))

        w_in = sb("w_in", [P, 2 * INNER_M])
        w_x = sb("w_x", [P, H2, 40])
        w_dt = sb("w_dt", [DT_RANK, INNER_M])
        w_out = sb("w_out", [P, H2, DIM])
        pick = sb("pick", [32, 32, P])
        ident = sb("m_ident", [P, P])
        vec = sb("m_vec", [P, 32])
        alog = sb("alog", [P, H2, STATE])
        aneg = sb("aneg", [P, H2, STATE])
        aexp = sb("aexp", [P, H2, STATE])
        xi = sb("xi", [P, H2, CONV - 1 + CH])
        zs = sb("zs", [P, H2, CH])
        cv = [sb(f"cv{i}", [P, H2, CH]) for i in range(2)]
        xc = sb("xc", [P, H2, CH])
        dt = sb("dt", [P, H2, CH])
        dtx = sb("dtx", [P, H2, CH])
        t_a = sb("t_a", [P, H2, CH])
        t_e = sb("t_e", [P, H2, CH])
        t_u = sb("t_u", [P, H2, CH])
        t_l = sb("t_l", [P, H2, CH])
        t_i = sb("t_i", [P, H2, CH])
        t_m = sb("t_m", [P, H2, CH])
        lr = sb("lr", [DT_RANK, CH])
        bc = sb("bc", [32, CH])
        bsp = sb("bsp", [P, 2, CH])
        dA = sb("dA", [P, 2, H2, CH])
        dBu = sb("dBu", [P, 2, H2, CH])
        hs = sb("hs", [P, 2, H2, CH])
        hc = sb("hc", [P, 2, H2, CH])
        state = sb("state", [P, STATE, H2])
        yg = sb("yg", [P, H2, CH])
        y2 = sb("y2", [P, H2, CH])
        so = sb("so", [P, CH])
        ps_a = psum("ps_a", [P, H2, 512])
        ps_b = [psum(f"ps_b{i}", [P, 512]) for i in range(2)]
        ps_c = [psum(f"ps_c{i}", [P, 512]) for i in range(2)]
        ps_y = psum("ps_y", [P, H2, 512])

        loaded = sem("m_loaded")
        a_ready = sem("a_ready")
        px_full = sem("px_full")
        px_free = sem("px_free")
        tail_kept = sem("tail_kept")
        conv_step = sem("conv_step")
        xc_ready = sem("xc_ready")
        bc_ready = sem("bc_ready")
        sp_act = sem("sp_act")
        sp_dve = sem("sp_dve")
        dtx_ready = sem("dtx_ready")
        b_full, c_full = sem("b_full"), sem("c_full")
        b_copied = sem("b_copied")
        da_ready, dbu_ready = sem("da_ready"), sem("dbu_ready")
        scanned = sem("scanned")
        kept = sem("state_kept")
        hc_ready = sem("hc_ready")
        y_added = sem("y_added")
        y_step = sem("y_step")
        stored = sem("s_stored")
        so_ready = sem("so_ready")
        zeroed = sem("m_zeroed")
        spare = sem("m_spare")
        block = ctx.enter_context(nc.Block())

        NLOAD = 8

        @block.sync
        def _(sp):
            for dst, src in ((w_in, "w_in"), (w_x, "w_x"), (w_dt, "w_dt"), (w_out, "w_out"), (pick, "pick"),
                             (ident, "identity"), (vec, "m_vec"), (alog, "alog")):
                sp.dma_start(dst[:], d[src]).then_inc(loaded, 16)
            with sp.Fori(0, BATCH) as b:
                with sp.Fori(0, NCH) as c:
                    it = b * NCH + c
                    sp.wait_ge(so_ready, it + 1)
                    sp.dma_start(s_dram[:, bass.ds(it * CH, CH)], so[:]).then_inc(stored, 16)
            sp.wait_ge(stored, 16 * BATCH * NCH)

        @block.tensor
        def _(pe):
            pe.wait_ge(loaded, 16 * NLOAD)
            with pe.Fori(0, BATCH) as b:
                with pe.Fori(0, NCH) as c:
                    it = b * NCH + c
                    src = xt[:, bass.ds(b * ROW + c * CH + PAD, CH)]
                    for use in range(2):
                        if use == 0:
                            pe.wait_ge(so_ready, it)
                        else:
                            pe.wait_ge(px_free, it * 4 + 1)
                        for h in range(H2):
                            k = use * H2 + h
                            last = nc.tensor.matmul(ps_a[:, h, :], w_in[:, P * k:P * (k + 1)], src, start=True, stop=True)
                        last.then_inc(px_full, 1)
                    pe.wait_ge(px_free, it * 4 + 2)
                    pe.wait_ge(xc_ready, it + 1)
                    for h in range(H2):
                        nc.tensor.matmul(ps_a[0:DT_RANK, 0, :], w_x[:, h, 0:DT_RANK], xc[:, h, :],
                                         start=(h == 0), stop=(h == H2 - 1))
                    for h in range(H2):
                        last = nc.tensor.matmul(ps_a[0:32, 1, :], w_x[:, h, DT_RANK:40], xc[:, h, :],
                                                start=(h == 0), stop=(h == H2 - 1))
                    last.then_inc(px_full, 1)
                    pe.wait_ge(px_free, it * 4 + 3)
                    for h in range(H2):
                        last = nc.tensor.matmul(ps_a[:, h, :], w_dt[:, P * h:P * (h + 1)], lr[:], start=True, stop=True)
                    last.then_inc(px_full, 1)

                    def spread(n):
                        if n == 0:
                            pe.wait_ge(bc_ready, it + 1)
                        pe.wait_ge(b_copied, it * STATE + max(n - 1, 0))
                        nc.tensor.matmul(ps_b[n % 2][:], pick[:, n, :], bc[:], start=True, stop=True).then_inc(b_full, 1)
                        pe.wait_ge(hc_ready, it * STATE + max(n - 1, 0))
                        nc.tensor.matmul(ps_c[n % 2][:], pick[:, STATE + n, :], bc[:], start=True, stop=True).then_inc(c_full, 1)

                    def add(n):
                        pe.wait_ge(hc_ready, it * STATE + n + 1)
                        if n == 0:
                            pe.wait_ge(y_step, it * 2)
                        for h in range(H2):
                            last = nc.tensor.matmul(ps_y[:, h, :], ident[:], hc[:, n % 2, h, :],
                                                    start=(n == 0), stop=(n == STATE - 1))
                        last.then_inc(y_added, 1)

                    spread(0)
                    spread(1)
                    for n in range(STATE):
                        add(n)
                        if n + 2 < STATE:
                            spread(n + 2)
                    pe.wait_ge(px_free, it * 4 + 4)
                    pe.wait_ge(y_step, it * 2 + 2)
                    for h in range(H2):
                        last = nc.tensor.matmul(ps_a[:, 0, :], w_out[:, h, :], y2[:, h, :],
                                                start=(h == 0), stop=(h == H2 - 1))
                    last.then_inc(px_full, 1)

        @block.scalar
        def _(act):
            act.wait_ge(loaded, 16 * NLOAD)
            nc.scalar.activation(aexp[:], alog[:], ACT.Exp).then_inc(a_ready, 1)
            act.wait_ge(a_ready, 1)
            nc.scalar.mul(aneg[:], aexp[:], -1.0).then_inc(a_ready, 1)
            act.wait_ge(a_ready, 2)
            with act.Fori(0, BATCH) as b:
                with act.Fori(0, NCH) as c:
                    it = b * NCH + c
                    act.wait_ge(px_full, it * 5 + 1)
                    act.wait_ge(tail_kept, it + 1)
                    for h in range(H2):
                        last = nc.scalar.activation(xi[:, h, CONV - 1:], ps_a[:, h, :], ACT.Identity, bias=vec[:, h:h + 1])
                    last.then_inc(px_free, 1)
                    act.wait_ge(px_full, it * 5 + 2)
                    act.wait_ge(y_step, it * 2)
                    for h in range(H2):
                        last = nc.scalar.activation(zs[:, h, :], ps_a[:, h, :], ACT.Silu, bias=vec[:, 2 + h:3 + h])
                    last.then_inc(px_free, 1)
                    act.wait_ge(conv_step, (it + 1) * CONV * H2)
                    for h in range(H2):
                        last = nc.scalar.activation(xc[:, h, :], cv[(CONV - 1) % 2][:, h, :], ACT.Silu, bias=vec[:, 4 + h:5 + h])
                    last.then_inc(xc_ready, 1)
                    act.wait_ge(px_full, it * 5 + 3)
                    nc.scalar.copy(bc[:], ps_a[0:32, 1, :]).then_inc(bc_ready, 1)
                    nc.scalar.copy(lr[:], ps_a[0:DT_RANK, 0, :]).then_inc(px_free, 1)
                    act.wait_ge(px_full, it * 5 + 4)
                    act.wait_ge(dtx_ready, it)
                    for h in range(H2):
                        last = nc.scalar.activation(t_a[:, h, :], ps_a[:, h, :], ACT.Abs, bias=vec[:, 6 + h:7 + h])
                    last.then_inc(sp_act, 1)
                    act.wait_ge(sp_act, it * 4 + 1)
                    nc.scalar.activation(t_e[:], t_a[:], ACT.Exp, scale=-1.0).then_inc(sp_act, 1)
                    act.wait_ge(sp_dve, it * 5 + 1)
                    nc.scalar.activation(t_l[:], t_u[:], ACT.Ln).then_inc(sp_act, 1)
                    act.wait_ge(sp_act, it * 4 + 3)
                    nc.scalar.activation(t_i[:], t_l[:], ACT.Exp, scale=-1.0).then_inc(sp_act, 1)

                    def decay(n):
                        act.wait_ge(scanned, it * STATE + max(n - 1, 0))
                        for h in range(H2):
                            last = nc.scalar.activation(dA[:, n % 2, h, :], dt[:, h, :], ACT.Exp, scale=aneg[:, h, n:n + 1])
                        last.then_inc(da_ready, 1)

                    def take_b(n):
                        act.wait_ge(b_full, it * STATE + n + 1)
                        act.wait_ge(dbu_ready, it * STATE + max(n - 1, 0))
                        nc.scalar.copy(bsp[:, n % 2, :], ps_b[n % 2][:]).then_inc(b_copied, 1)

                    act.wait_ge(sp_dve, it * 5 + 5)
                    for n in range(STATE):
                        take_b(n)
                        decay(n)
                    act.wait_ge(px_full, it * 5 + 5)
                    act.wait_ge(stored, it * 16)
                    nc.scalar.activation(so[:], ps_a[:, 0, :], ACT.Identity, bias=vec[:, 10:11]).then_inc(so_ready, 1)

        @block.gpsimd
        def _(pool):
            with pool.Fori(0, BATCH) as b:
                with pool.Fori(0, NCH) as c:
                    it = b * NCH + c
                    pool.wait_ge(dtx_ready, it + 1)
                    for n in range(STATE):
                        pool.wait_ge(b_copied, it * STATE + n + 1)
                        pool.wait_ge(scanned, it * STATE + max(n - 1, 0))
                        nc.gpsimd.tensor_tensor(dBu[:, n % 2], dtx[:], bsp[:, n % 2, :].unsqueeze(1).broadcast_to([P, H2, CH]),
                                                ALU.mult).then_inc(dbu_ready, 1)

        @block.vector
        def _(dve):
            dve.wait_ge(loaded, 16 * NLOAD)
            with dve.Fori(0, BATCH) as b:
                dve.wait_ge(kept, b * NCH * STATE)
                nc.vector.memset(state[:], 0.0).then_inc(zeroed, 1)
                nc.vector.memset(xi[:, :, CH:CH + CONV - 1], 0.0).then_inc(zeroed, 1)
                wait_alone(dve, zeroed, 2 * b + 2, spare)
                with dve.Fori(0, NCH) as c:
                    it = b * NCH + c
                    dve.wait_ge(conv_step, it * CONV * H2)
                    nc.vector.tensor_copy(xi[:, :, 0:CONV - 1], xi[:, :, CH:CH + CONV - 1]).then_inc(tail_kept, 1)
                    dve.wait_ge(px_free, it * 4 + 1)
                    for k in range(CONV):
                        if k:
                            dve.wait_ge(conv_step, it * CONV * H2 + k * H2)
                        else:
                            dve.wait_ge(xc_ready, it)
                        for h in range(H2):
                            tap = vec[:, 12 + CONV * h + k:13 + CONV * h + k]
                            seen = xi[:, h, k:k + CH]
                            if k == 0:
                                i = nc.vector.tensor_scalar(cv[0][:, h, :], seen, tap, None, ALU.mult)
                            else:
                                i = nc.vector.scalar_tensor_tensor(out=cv[k % 2][:, h, :], in0=seen, scalar=tap,
                                                                   in1=cv[(k - 1) % 2][:, h, :], op0=ALU.mult, op1=ALU.add)
                            i.then_inc(conv_step, 1)
                    dve.wait_ge(sp_act, it * 4 + 1)
                    for h in range(H2):
                        i = nc.vector.tensor_scalar(t_m[:, h, :], ps_a[:, h, :], vec[:, 6 + h:7 + h], 0.0, ALU.add, ALU.max)
                    i.then_inc(px_free, 1)
                    dve.wait_ge(sp_act, it * 4 + 2)
                    nc.vector.tensor_scalar(t_u[:], t_e[:], 1.0, None, ALU.add).then_inc(sp_dve, 1)
                    dve.wait_ge(sp_dve, it * 5 + 1)
                    nc.vector.scalar_tensor_tensor(out=t_e[:], in0=t_u[:], scalar=-1.0, in1=t_e[:], op0=ALU.add,
                                                   op1=ALU.subtract).then_inc(sp_dve, 1)
                    dve.wait_ge(sp_dve, it * 5 + 2)
                    dve.wait_ge(sp_act, it * 4 + 4)
                    nc.vector.tensor_tensor(t_e[:], t_e[:], t_i[:], ALU.mult).then_inc(sp_dve, 1)
                    dve.wait_ge(sp_dve, it * 5 + 3)
                    nc.vector.tensor_tensor(t_m[:], t_m[:], t_e[:], ALU.subtract).then_inc(sp_dve, 1)
                    dve.wait_ge(sp_dve, it * 5 + 4)
                    dve.wait_ge(da_ready, it * STATE)
                    nc.vector.tensor_tensor(dt[:], t_m[:], t_l[:], ALU.add).then_inc(sp_dve, 1)
                    dve.wait_ge(sp_dve, it * 5 + 5)
                    dve.wait_ge(dbu_ready, it * STATE)
                    nc.vector.tensor_tensor(dtx[:], dt[:], xc[:], ALU.mult).then_inc(dtx_ready, 1)
                    for n in range(STATE):
                        dve.wait_ge(da_ready, it * STATE + n + 1)
                        dve.wait_ge(dbu_ready, it * STATE + n + 1)
                        dve.wait_ge(hc_ready, it * STATE + max(n - 1, 0))
                        dve.wait_ge(kept, it * STATE + n)
                        for h in range(H2):
                            i = nc.vector.tensor_tensor_scan(hs[:, n % 2, h, :], dA[:, n % 2, h, :], dBu[:, n % 2, h, :],
                                                             state[:, n, h:h + 1], ALU.mult, ALU.add)
                        i.then_inc(scanned, 1)
                        dve.wait_ge(scanned, it * STATE + n + 1)
                        nc.vector.tensor_copy(state[:, n, :], hs[:, n % 2, :, CH - 1]).then_inc(kept, 1)
                        dve.wait_ge(c_full, it * STATE + n + 1)
                        dve.wait_ge(y_added, it * STATE + max(n - 1, 0))
                        nc.vector.tensor_tensor(hc[:, n % 2], hs[:, n % 2], ps_c[n % 2][:].unsqueeze(1).broadcast_to([P, H2, CH]),
                                                ALU.mult).then_inc(hc_ready, 1)
                    dve.wait_ge(y_added, (it + 1) * STATE)
                    for h in range(H2):
                        i = nc.vector.scalar_tensor_tensor(out=yg[:, h, :], in0=xc[:, h, :], scalar=vec[:, 8 + h:9 + h],
                                                           in1=ps_y[:, h, :], op0=ALU.mult, op1=ALU.add)
                    i.then_inc(y_step, 1)
                    dve.wait_ge(y_step, it * 2 + 1)
                    dve.wait_ge(px_full, it * 5)
                    nc.vector.tensor_tensor(y2[:], yg[:], zs[:], ALU.mult).then_inc(y_step, 1)


def jobs_of_a_turn():
    order = []
    for s in range(UNITS + 1):
        if s < UNITS:
            order += [("qk", s, 0), ("qk", s, 1)]
        if s >= 1:
            order.append(("norm", s - 1, 0))
        if s < UNITS:
            order += [("qk", s, 2), ("qk", s, 3)]
        if s in (1, 3):
            order += [("v", s // 2, i) for i in range(4)]
    order += [("wo", b, 0) for b in range(BATCH)]
    return order + [("mean", 0, 0), ("var", 0, 0), ("hidden", 0, 0), ("hidden", 1, 0), ("hidden", 2, 0), ("out", 0, 0)]


JOBS = jobs_of_a_turn()
assert len(JOBS) % 2 == 0
PER_SLOT = len(JOBS) // 2


def phase_layers(nc, xt, d):
    with ExitStack() as ctx:
        def sb(name, shape, dt=F32):
            return ctx.enter_context(nc.sbuf_tensor(name, shape, dt))

        def sem(name):
            return ctx.enter_context(nc.semaphore(name))

        wqk = sb("wqk", [P, 2, 8, 2, P])
        wv = sb("wv", [P, INNER])
        wo = sb("wo", [P, 8, DIM])
        w1 = sb("w1", [P, 2 * FF])
        w2 = sb("w2", [P, 3, DIM])
        par = sb("par", [P, NPAR])
        tabs = sb("tabs", [P, TAB])
        tab = tabs[:, 0:4 * TILE].rearrange("p (k t) -> p k t", k=4)
        flag = tabs[:, 4 * TILE:TAB]
        mask = sb("mask", [P, 512], BF16)
        mask0 = sb("mask0", [P, NT * 2 * WIN], BF16)
        ident_b = sb("ident_b", [P, P], BF16)
        ident = sb("l_ident", [P, P])
        ones_half = sb("ones_half", [P, 2, WIN])
        halves = sb("halves", [P, 2])
        mean_w = sb("mean_w", [P, P])
        small = sb("small", [P, 2])
        xin = sb("xin", [P, BATCH, HALO + TILE])
        t_qk = sb("t_qk", [P, 2, 2, 2, TILE])
        qr = sb("qr", [P, 2, 4, TILE])
        kr = sb("kr", [P, UNITS, 4, HALO + TILE])
        sqs = sb("sqs", [P, 2, 2, 4, TILE])
        kss = sb("kss", [P, 2, 512])
        qss = sb("qss", [P, 2, 2 * NWIN])
        kinv = sb("kinv", [P, UNITS, 2, HALO + TILE])
        qinv = sb("qinv", [P, 2, 2 * NWIN])
        pr = sb("pr", [P, 2, 2, 512])
        smax = sb("smax", [P, 2, 2 * NWIN])
        ssum = sb("ssum", [P, 2, 2 * NWIN])
        sinv = sb("sinv", [P, 2, 2 * NWIN])
        prt = sb("prt", [P, 2, 2, 512])
        vals = sb("vals", [P, 4, INNER])
        ot = sb("ot", [P, BATCH, 2, 2, 4, P])
        x1 = sb("x1", [P, BATCH, 1 + TILE])
        xf = sb("xf", [P, BATCH, TILE])
        xc = sb("l_xc", [P, BATCH, TILE])
        xsq = sb("xsq", [P, 512])
        rstd = sb("l_rstd", [P, 512])
        xn = sb("xn", [P, 2, 512])
        gate = sb("gate", [P, 3, 512])
        ring = [ctx.enter_context(nc.psum_tensor(f"ring{i}", [P, 2, 512], F32)) for i in range(2)]
        ps_s = ctx.enter_context(nc.psum_tensor("ps_s", [P, 2, 512], F32))
        ps_p = ctx.enter_context(nc.psum_tensor("ps_p", [P, 2, 512], F32))

        consts = sem("consts")
        cleared = sem("cleared")
        wqk_in, wv_in, wo_in, wf_in = sem("wqk_in"), sem("wv_in"), sem("wo_in"), sem("wf_in")
        tab_in = sem("tab_in")
        xin_ready = sem("xin_ready")
        full = [sem(f"slot{i}_full") for i in range(2)]
        free = [sem(f"slot{i}_free") for i in range(2)]
        squared = sem("l_squared")
        added = sem("added")
        halo_moved = sem("halo_moved")
        inv_step = sem("inv_step")
        inv_ready = sem("inv_ready")
        scores_done = sem("scores_done")
        sm_step = sem("sm_step")
        q_scaled = sem("q_scaled")
        exp_done = sem("exp_done")
        sum_step = sem("sum_step")
        p_normed = sem("p_normed")
        turned = sem("l_turned")
        turned_read = sem("turned_read")
        pv_done = sem("pv_done")
        ot_ready = sem("ot_ready")
        x1_step = sem("x1_step")
        ff_dve = sem("ff_dve")
        ff_act = sem("ff_act")
        gated = sem("gated")
        spare = {e: sem(f"spare_{e}") for e in ("pe", "pool", "dve")}
        block = ctx.enter_context(nc.Block())
        NCONST = 8

        def slot_of(job):
            n = JOBS.index(job)
            return n % 2, n // 2

        def wait_full(eng, it, job):
            s, m = slot_of(job)
            eng.wait_ge(full[s], it * PER_SLOT + m + 1)

        def wait_taken(eng, it, job):
            s, m = slot_of(job)
            eng.wait_ge(free[s], it * PER_SLOT + m + 1)

        def wait_turns(eng, turns):
            eng.wait_ge(free[1], turns * PER_SLOT)

        def wait_free(pe, it, job):
            s, m = slot_of(job)
            pe.wait_ge(free[s], it * PER_SLOT + m)

        def unit(s):
            return s // 2, s % 2

        def used(it, s):
            return it * UNITS + max(s - 1, 0)

        @block.sync
        def _(sp):
            for dst, src in ((mask, "mask"), (mask0, "mask0"), (ident_b, "identity_b"), (ident, "identity"),
                             (ones_half, "ones_half"), (halves, "halves"), (mean_w, "mean_w"), (small, "small")):
                sp.dma_start(dst[:], d[src]).then_inc(consts, 16)
            with sp.Fori(0, DEPTH) as l:
                sp.wait_ge(added, l * NT * 16)
                sp.dma_start(wqk[:], d["wqk"][:, bass.ds(l * 4096, 4096)]).then_inc(wqk_in, 16)
                sp.wait_ge(ot_ready, l * NT * UNITS)
                sp.dma_start(wv[:], d["wv"][:, bass.ds(l * INNER, INNER)]).then_inc(wv_in, 16)
                sp.wait_ge(ff_dve, l * NT * 4)
                sp.dma_start(wo[:], d["wo"][:, bass.ds(l * 8 * DIM, 8 * DIM)]).then_inc(wo_in, 16)
                wait_turns(sp, l * NT)
                sp.dma_start(w1[:], d["w1"][:, bass.ds(l * 2 * FF, 2 * FF)]).then_inc(wf_in, 16)
                sp.dma_start(w2[:], d["w2"][:, bass.ds(l * 3 * DIM, 3 * DIM)]).then_inc(wf_in, 16)
                sp.dma_start(par[:], d["par"][:, bass.ds(l * NPAR, NPAR)]).then_inc(wf_in, 16)
                with sp.Fori(0, NT) as i:
                    it = l * NT + i
                    sp.wait_ge(x1_step, it * 4)
                    sp.dma_start(tabs[:], d["tables"][:, bass.ds(i * TAB, TAB)]).then_inc(tab_in, 16)

        @block.tensor
        def _(pe):
            def qk(it, s, j):
                b, o = unit(s)
                wait_free(pe, it, ("qk", s, j))
                ps = ring[slot_of(("qk", s, j))[0]]
                for part in range(2):
                    for c in range(2):
                        last = nc.tensor.matmul(ps[:, part, TILE * c:TILE * (c + 1)], wqk[:, j // 2, 4 * o + 2 * (j % 2) + c, part, :],
                                                xin[:, b, HALO:], start=True, stop=True)
                last.then_inc(full[slot_of(("qk", s, j))[0]], 1)

            def norm(it, s):
                b, o = unit(s)
                wait_free(pe, it, ("norm", s, 0))
                slot = slot_of(("norm", s, 0))[0]
                ps = ring[slot]
                pe.wait_ge(squared, it * 16 + 4 * s + 4)
                for c in range(4):
                    for half in range(2):
                        nc.tensor.matmul(ps[32 * c:32 * c + 32, 0, TILE * half:TILE * (half + 1)], ones_half[:, half, :],
                                         sqs[:, s % 2, 1, c, :], start=True, stop=True)
                for c in range(4):
                    for w in range(NWIN):
                        p = pos(w)
                        last = nc.tensor.matmul(ps[32 * c:32 * c + 32, 1, 2 * p:2 * p + 2],
                                                sqs[:, s % 2, 0, c, WIN * w:WIN * (w + 1)], halves[:], start=True, stop=True)
                last.then_inc(full[slot], 1)

            def scores(it, i, s):
                pe.wait_ge(sm_step, it * UNITS * 4 + max(4 * s - 2, 0))
                pe.wait_ge(added, it * 16 + 4 * s + 4)
                for half in range(2):
                    nc.tensor.matmul(ps_s[:, half, 2 * WIN:], ident_b[:], mask[:, 2 * WIN:], start=True, stop=False,
                                     skip_group_check=True)
                    nc.tensor.matmul(ps_s[:, half, 0:2 * WIN], ident_b[:], mask0[:, bass.ds(i * 2 * WIN, 2 * WIN)], start=False, stop=False,
                                     skip_group_check=True)
                for c in range(4):
                    for w in range(NWIN):
                        for half in range(2):
                            r = slice(64 * half, 64 * half + 64)
                            last = nc.tensor.matmul(ps_s[32 * c:32 * c + 32, half, 64 * pos(w):64 * pos(w) + 64],
                                                    qr[r, s % 2, c, WIN * w:WIN * (w + 1)],
                                                    kr[r, s, c, WIN * w:WIN * (w + 2)], start=False, stop=True,
                                                    skip_group_check=True)
                last.then_inc(scores_done, 1)

            def value(it, b):
                for i in range(4):
                    job = ("v", b, i)
                    wait_free(pe, it, job)
                    slot = slot_of(job)[0]
                    first = P * (i % 2) + (HALO if i >= 2 else 0)
                    for n in range(2):
                        last = nc.tensor.matmul(ring[slot][:, n, :], xin[:, b, first:first + P], wv[:, 512 * n:512 * (n + 1)],
                                                start=True, stop=True)
                    last.then_inc(full[slot], 1)

            def turn(it, s):
                pe.wait_ge(p_normed, it * UNITS + s + 1)
                pe.wait_ge(ot_ready, it * UNITS + s)
                for half in range(2):
                    for k in range(4):
                        last = nc.tensor.transpose(ps_p[:, half, P * k:P * (k + 1)], pr[:, s % 2, half, P * k:P * (k + 1)], ident[:])
                last.then_inc(turned, 1)

            def weigh(it, s):
                b, o = unit(s)
                wait_taken(pe, it, ("v", b, 2))
                wait_taken(pe, it, ("v", b, 3))
                wait_alone(pe, turned_read, it * UNITS + s + 1, spare["pe"])
                for c in range(4):
                    for k in range(4):
                        for half in range(2):
                            for lower in range(2):
                                r = slice(64 * lower, 64 * lower + 64)
                                head = 8 * o + 2 * c + half
                                last = nc.tensor.matmul(ps_p[64 * half:64 * half + 64, lower, P * c + 32 * k:P * c + 32 * k + 32],
                                                        vals[r, k, DH * head:DH * (head + 1)],
                                                        prt[r, s % 2, half, P * k + 32 * c:P * k + 32 * c + 32],
                                                        start=True, stop=True)
                last.then_inc(pv_done, 1)

            def project(it, b):
                job = ("wo", b, 0)
                wait_free(pe, it, job)
                slot = slot_of(job)[0]
                pe.wait_ge(ot_ready, it * UNITS + 2 * b + 2)
                for o in range(2):
                    for c in range(4):
                        last = nc.tensor.matmul(ring[slot][:, 0, 0:TILE], wo[:, 4 * o + c, :], ot[:, b, o, :, c, :],
                                                start=(o + c == 0), stop=(o + c == 4))
                last.then_inc(full[slot], 1)

            def hidden(it, l):
                for name in ("mean", "var"):
                    wait_free(pe, it, (name, 0, 0))
                    slot = slot_of((name, 0, 0))[0]
                    if name == "mean":
                        pe.wait_ge(ff_dve, it * 4 + 2)
                    else:
                        pe.wait_ge(ff_act, it * 2 + 1)
                    nc.tensor.matmul(ring[slot][:, 0, :], mean_w[:], xf[:] if name == "mean" else xsq[:],
                                     start=True, stop=True).then_inc(full[slot], 1)
                pe.wait_ge(wf_in, 48 * l + 48)
                for c in range(3):
                    job = ("hidden", c, 0)
                    wait_free(pe, it, job)
                    slot = slot_of(job)[0]
                    if c == 0:
                        pe.wait_ge(ff_dve, it * 4 + 4)
                    m = P if c < 2 else FFR
                    for part in range(2):
                        last = nc.tensor.matmul(ring[slot][0:m, part, :], w1[:, FF * part + P * c:FF * part + P * c + m],
                                                xn[:, 1, :], start=True, stop=True)
                    last.then_inc(full[slot], 1)
                job = ("out", 0, 0)
                wait_free(pe, it, job)
                slot = slot_of(job)[0]
                wait_taken(pe, it, ("hidden", 1, 0))
                wait_taken(pe, it, ("hidden", 2, 0))
                for c in range(3):
                    m = P if c < 2 else FFR
                    last = nc.tensor.matmul(ring[slot][:, 0, :], w2[0:m, c, :], gate[0:m, c, :], start=(c == 0), stop=(c == 2))
                last.then_inc(full[slot], 1)

            pe.wait_ge(consts, 16 * NCONST)
            pe.wait_ge(cleared, 3)
            with pe.Fori(0, DEPTH) as l:
                pe.wait_ge(wqk_in, 16 * l + 16)
                pe.wait_ge(wv_in, 16 * l + 16)
                wait_alone(pe, wo_in, 16 * l + 16, spare["pe"])
                with pe.Fori(0, NT) as i:
                    it = l * NT + i
                    pe.wait_ge(xin_ready, it * 4 + 4)
                    for s in range(UNITS + 2):
                        if s < UNITS:
                            qk(it, s, 0)
                            qk(it, s, 1)
                        if 1 <= s <= UNITS:
                            norm(it, s - 1)
                        if s < UNITS:
                            qk(it, s, 2)
                        if 1 <= s <= UNITS:
                            scores(it, i, s - 1)
                        if s >= 2:
                            turn(it, s - 2)
                        if s < UNITS:
                            qk(it, s, 3)
                        if s >= 2:
                            weigh(it, s - 2)
                        if s in (1, 3):
                            value(it, s // 2)
                    for b in range(BATCH):
                        project(it, b)
                    hidden(it, l)

        @block.scalar
        def _(act):
            def square(it, s, j):
                wait_full(act, it, ("qk", s, j))
                ps = ring[slot_of(("qk", s, j))[0]]
                nc.scalar.activation(sqs[:, s % 2, j // 2, 2 * (j % 2):2 * (j % 2) + 2, :], ps[:, 0, :], ACT.Square).then_inc(squared, 1)

            def invert(it, s):
                wait_taken(act, it, ("norm", s, 0))
                nc.scalar.activation(kss[:, s % 2, :], kss[:, s % 2, :], ACT.Ln, scale=float(2 ** LN_SHIFT)).then_inc(inv_step, 1)
                nc.scalar.activation(qss[:, s % 2, :], qss[:, s % 2, :], ACT.Ln, scale=float(2 ** LN_SHIFT)).then_inc(inv_step, 1)
                act.wait_ge(inv_step, (it * UNITS + s) * 2 + 2)
                act.wait_ge(halo_moved, it * UNITS * 2 + 2 * s + 2)
                act.wait_ge(q_scaled, used(it, s))
                nc.scalar.activation(kinv[:, s, :, HALO:], kss[:, s % 2, :], ACT.Exp, scale=-0.5, bias=small[:, 1:2]).then_inc(inv_ready, 1)
                nc.scalar.activation(qinv[:, s % 2, :], qss[:, s % 2, :], ACT.Exp, scale=-0.5, bias=small[:, 1:2]).then_inc(inv_ready, 1)

            def exps(it, s):
                act.wait_ge(q_scaled, it * UNITS + s + 1)
                nc.scalar.activation(pr[:, s % 2], pr[:, s % 2], ACT.Exp, scale=QK_SCALE).then_inc(exp_done, 1)

            def values(it, b):
                for i in range(4):
                    wait_full(act, it, ("v", b, i))
                    if i == 0:
                        act.wait_ge(pv_done, it * UNITS + 2 * b)
                    slot = slot_of(("v", b, i))[0]
                    nc.scalar.copy(vals[:, i, :], ring[slot][:]).then_inc(free[slot], 1)

            def take_turned(it, s):
                act.wait_ge(turned, it * UNITS + s + 1)
                act.wait_ge(pv_done, used(it, s))
                nc.scalar.copy(prt[:, s % 2], ps_p[:]).then_inc(turned_read, 1)

            def take_out(it, s):
                b, o = unit(s)
                act.wait_ge(pv_done, it * UNITS + s + 1)
                nc.scalar.copy(ot[:, b, o], ps_p[:]).then_inc(ot_ready, 1)

            act.wait_ge(consts, 16 * NCONST)
            with act.Fori(0, DEPTH) as l:
                with act.Fori(0, NT) as i:
                    it = l * NT + i
                    for s in range(UNITS + 2):
                        if s < UNITS:
                            square(it, s, 0)
                            square(it, s, 1)
                        if 1 <= s <= UNITS:
                            invert(it, s - 1)
                        if s < UNITS:
                            square(it, s, 2)
                        if s >= 2:
                            take_turned(it, s - 2)
                        if s < UNITS:
                            square(it, s, 3)
                        if s >= 2:
                            take_out(it, s - 2)
                        if s in (1, 3):
                            values(it, s // 2)
                        if 1 <= s <= UNITS:
                            exps(it, s - 1)
                    wait_taken(act, it, ("mean", 0, 0))
                    nc.scalar.activation(xsq[:], xc[:], ACT.Square).then_inc(ff_act, 1)
                    wait_full(act, it, ("var", 0, 0))
                    slot = slot_of(("var", 0, 0))[0]
                    nc.scalar.activation(rstd[:], ring[slot][:, 0, :], ACT.Ln, bias=small[:, 0:1]).then_inc(free[slot], 1)
                    wait_taken(act, it, ("var", 0, 0))
                    nc.scalar.activation(rstd[:], rstd[:], ACT.Exp, scale=-0.5).then_inc(ff_act, 1)
                    for c in range(3):
                        m = P if c < 2 else FFR
                        wait_full(act, it, ("hidden", c, 0))
                        nc.scalar.activation(gate[0:m, c, :], ring[slot_of(("hidden", c, 0))[0]][0:m, 1, :], ACT.Gelu,
                                             bias=par[0:m, B1G + c:B1G + c + 1]).then_inc(gated, 1)

        @block.gpsimd
        def _(pool):
            for t in (kr, kinv):
                nc.gpsimd.memset(t[:], 1.0).then_inc(cleared, 1)
            nc.gpsimd.memset(x1[:], 0.0).then_inc(cleared, 1)
            pool.wait_ge(cleared, 3)

            def keep_halo(it, s):
                wait_alone(pool, scores_done, it * UNITS, spare["pool"])
                nc.gpsimd.tensor_scalar(kr[:, s, :, 0:HALO], kr[:, s, :, TILE:], flag, 1.0, ALU.mult, ALU.mult).then_inc(halo_moved, 1)
                wait_alone(pool, sm_step, it * UNITS * 4, spare["pool"])
                nc.gpsimd.tensor_copy(kinv[:, s, :, 0:HALO], kinv[:, s, :, TILE:]).then_inc(halo_moved, 1)

            def join(it, s, j):
                if j == 0:
                    pool.wait_ge(scores_done, used(it, s))
                if j == 2:
                    pool.wait_ge(halo_moved, it * UNITS * 2 + 2 * s + 2)
                wait_taken(pool, it, ("qk", s, j))
                c = 2 * (j % 2)
                dst = qr[:, s % 2, c:c + 2, :] if j < 2 else kr[:, s, c:c + 2, HALO:]
                nc.gpsimd.tensor_tensor(dst, t_qk[:, j % 2, 0], t_qk[:, j % 2, 1], ALU.add).then_inc(added, 1)

            def scale_q(it, s):
                pool.wait_ge(sm_step, (it * UNITS + s) * 4 + 4)
                pool.wait_ge(inv_ready, (it * UNITS + s) * 2 + 2)
                q = qinv[:, s % 2, :].rearrange("p (w h) -> p h w", h=2)
                for half in range(2):
                    v = pr[:, s % 2, half].rearrange("p (w k) -> p w k", k=2 * WIN)
                    last = nc.gpsimd.tensor_tensor(v, v, q[:, half, :].unsqueeze(2).broadcast_to([P, NWIN, 2 * WIN]), ALU.mult)
                last.then_inc(q_scaled, 1)

            def normalise(it, s):
                pool.wait_ge(sum_step, (it * UNITS + s) * 2 + 2)
                v = pr[:, s % 2].rearrange("p h (w k) -> p (h w) k", k=2 * WIN)
                nc.gpsimd.tensor_tensor(v, v, sinv[:, s % 2, :].unsqueeze(2).broadcast_to([P, 2 * NWIN, 2 * WIN]),
                                        ALU.mult).then_inc(p_normed, 1)

            with pool.Fori(0, DEPTH * NT) as it:
                wait_alone(pool, tab_in, 16 * it + 16, spare["pool"])
                for s in range(UNITS + 2):
                    if s < UNITS:
                        join(it, s, 0)
                        join(it, s, 1)
                    if s >= 2:
                        normalise(it, s - 2)
                    if s < UNITS:
                        keep_halo(it, s)
                        join(it, s, 2)
                        join(it, s, 3)
                    if 1 <= s <= UNITS:
                        scale_q(it, s - 1)

        @block.vector
        def _(dve):
            def shift_in(it, l, i):
                for b in range(BATCH):
                    for lower in range(2):
                        r = slice(64 * lower, 64 * lower + 64)
                        col = (l % 2) * (BATCH * ROW) + b * ROW + PAD - HALO - lower + i * TILE
                        i_ = nc.vector.tensor_copy(xin[r, b, :], xt[r, bass.ds(col, HALO + TILE)])
                        i_.then_inc(xin_ready, 1)

            def rotate(it, l, s, j):
                job = ("qk", s, j)
                ps = ring[slot_of(job)[0]]
                kq = j // 2
                wait_full(dve, it, job)
                g = it * 16 + 4 * s + j
                dve.wait_ge(added, it * 16 + max(4 * s + j - 1, 0))
                for part in (1, 0):
                    if part == 0:
                        dve.wait_ge(squared, g + 1)
                    t = nc.vector.scalar_tensor_tensor(
                        out=t_qk[:, j % 2, part], in0=ps[:, part, :].rearrange("p (c t) -> p c t", c=2),
                        scalar=par[:, 2 * kq + part:2 * kq + part + 1],
                        in1=tab[:, 2 * kq + part, :].unsqueeze(1).broadcast_to([P, 2, TILE]), op0=ALU.mult, op1=ALU.mult)
                    if part == 0:
                        t.then_inc(free[slot_of(job)[0]], 1)

            def read_norms(it, s):
                job = ("norm", s, 0)
                wait_full(dve, it, job)
                dve.wait_ge(inv_ready, used(it, s) * 2)
                slot = slot_of(job)[0]
                nc.vector.tensor_scalar(qss[:, s % 2, :], ring[slot][:, 1, 0:2 * NWIN], NORM_FLOOR ** 2, None, ALU.max)
                nc.vector.tensor_scalar(kss[:, s % 2, :], ring[slot][:, 0, :], NORM_FLOOR ** 2, None,
                                        ALU.max).then_inc(free[slot], 1)

            def softmax_top(it, s):
                n = it * UNITS + s
                dve.wait_ge(scores_done, n + 1)
                dve.wait_ge(inv_ready, n * 2 + 1)
                dve.wait_ge(turned, used(it, s))
                for half in range(2):
                    kv = kinv[:, s, half, :]
                    for c in range(2):
                        keys = bass.AP(kv.tensor, kv.offset + WIN * c, [kv.ap[0], [2 * WIN, 4], [1, 2 * WIN]])
                        cols = slice(4 * 2 * WIN * c, 4 * 2 * WIN * (c + 1))
                        last = nc.vector.tensor_tensor(pr[:, s % 2, half, cols].rearrange("p (w k) -> p w k", k=2 * WIN),
                                                       ps_s[:, half, cols].rearrange("p (w k) -> p w k", k=2 * WIN),
                                                       keys, ALU.mult)
                    last.then_inc(sm_step, 1)
                v = pr[:, s % 2].rearrange("p h (w k) -> p (h w) k", k=2 * WIN)
                dve.wait_ge(sm_step, n * 4 + 2)
                nc.vector.tensor_reduce(smax[:, s % 2, :], v, AX_X, ALU.max).then_inc(sm_step, 1)
                dve.wait_ge(sm_step, n * 4 + 3)
                nc.vector.tensor_tensor(v, v, smax[:, s % 2, :].unsqueeze(2).broadcast_to([P, 2 * NWIN, 2 * WIN]),
                                        ALU.subtract).then_inc(sm_step, 1)

            def softmax_sum(it, s):
                n = it * UNITS + s
                dve.wait_ge(exp_done, n + 1)
                v = pr[:, s % 2].rearrange("p h (w k) -> p (h w) k", k=2 * WIN)
                nc.vector.tensor_reduce(ssum[:, s % 2, :], v, AX_X, ALU.add).then_inc(sum_step, 1)
                dve.wait_ge(sum_step, n * 2 + 1)
                nc.vector.reciprocal(sinv[:, s % 2, :], ssum[:, s % 2, :]).then_inc(sum_step, 1)

            def attention_sum(it, l, i, b):
                job = ("wo", b, 0)
                slot = slot_of(job)[0]
                nc.vector.tensor_scalar(x1[:, b, 0:1], x1[:, b, TILE:TILE + 1], flag, None, ALU.mult).then_inc(x1_step, 1)
                dve.wait_ge(x1_step, it * 4 + 2 * b + 1)
                wait_full(dve, it, job)
                for lower in range(2):
                    old = (l % 2) * (BATCH * ROW) + b * ROW + PAD + i * TILE
                    src = ring[slot][:, 0, P * lower:P * (lower + 1)].rearrange("p (a b t) -> p b a t", a=2, b=2)
                    x_old = xt[:, bass.ds(old, TILE)].rearrange("p (b l a t) -> p b l a t", b=2, l=2, a=2)[:, :, lower]
                    x_new = x1[:, b, 1:].rearrange("p (b l a t) -> p b l a t", b=2, l=2, a=2)[:, :, lower]
                    last = nc.vector.tensor_tensor(x_new, src, x_old, ALU.add)
                    last.then_inc(free[slot] if lower else x1_step, 1)

            def hidden(it, l, i):
                wait_taken(dve, it, ("wo", 0, 0))
                wait_taken(dve, it, ("wo", 1, 0))
                for lower in range(2):
                    r = slice(64 * lower, 64 * lower + 64)
                    nc.vector.tensor_copy(xf[r], x1[r, :, 1 - lower:1 - lower + TILE]).then_inc(ff_dve, 1)
                dve.wait_ge(ff_dve, it * 4 + 2)
                wait_full(dve, it, ("mean", 0, 0))
                slot = slot_of(("mean", 0, 0))[0]
                nc.vector.tensor_tensor(xc[:].rearrange("p b t -> p (b t)"), xf[:].rearrange("p b t -> p (b t)"),
                                        ring[slot][:, 0, :], ALU.subtract).then_inc(free[slot], 1)
                wait_taken(dve, it, ("mean", 0, 0))
                dve.wait_ge(ff_act, it * 2 + 2)
                nc.vector.scalar_tensor_tensor(out=xn[:, 0, :], in0=xc[:].rearrange("p b t -> p (b t)"), scalar=par[:, LG:LG + 1],
                                               in1=rstd[:], op0=ALU.mult, op1=ALU.mult).then_inc(ff_dve, 1)
                dve.wait_ge(ff_dve, it * 4 + 3)
                nc.vector.tensor_scalar(xn[:, 1, :], xn[:, 0, :], par[:, LB:LB + 1], None, ALU.add).then_inc(ff_dve, 1)
                for c in range(3):
                    m = P if c < 2 else FFR
                    wait_full(dve, it, ("hidden", c, 0))
                    dve.wait_ge(gated, it * 3 + c + 1)
                    slot = slot_of(("hidden", c, 0))[0]
                    nc.vector.scalar_tensor_tensor(out=gate[0:m, c, :], in0=ring[slot][0:m, 0, :], scalar=par[0:m, B1A + c:B1A + c + 1],
                                                   in1=gate[0:m, c, :], op0=ALU.add, op1=ALU.mult).then_inc(free[slot], 1)
                wait_full(dve, it, ("out", 0, 0))
                slot = slot_of(("out", 0, 0))[0]
                for b in range(BATCH):
                    new = ((l + 1) % 2) * (BATCH * ROW) + b * ROW + PAD + i * TILE
                    last = nc.vector.scalar_tensor_tensor(out=xt[:, bass.ds(new, TILE)], in0=ring[slot][:, 0, TILE * b:TILE * (b + 1)],
                                                          scalar=par[:, B2:B2 + 1], in1=x1[:, b, 1:], op0=ALU.add, op1=ALU.add)
                last.then_inc(free[slot], 1)

            dve.wait_ge(consts, 16 * NCONST)
            dve.wait_ge(cleared, 3)
            with dve.Fori(0, DEPTH) as l:
                wait_alone(dve, wf_in, 48 * l + 48, spare["dve"])
                with dve.Fori(0, NT) as i:
                    it = l * NT + i
                    wait_turns(dve, it)
                    shift_in(it, l, i)
                    dve.wait_ge(tab_in, 16 * it + 16)
                    for s in range(UNITS + 2):
                        if s < UNITS:
                            rotate(it, l, s, 0)
                            rotate(it, l, s, 1)
                        if 1 <= s <= UNITS:
                            read_norms(it, s - 1)
                        if s >= 2:
                            softmax_sum(it, s - 2)
                        if s < UNITS:
                            rotate(it, l, s, 2)
                        if 1 <= s <= UNITS:
                            softmax_top(it, s - 1)
                        if s < UNITS:
                            rotate(it, l, s, 3)
                    for b in range(BATCH):
                        attention_sum(it, l, i, b)
                    hidden(it, l, i)


def phase_join(nc, xt, x, s_dram, identity, out):
    with ExitStack() as ctx:
        def sb(name, shape, dt=F32):
            return ctx.enter_context(nc.sbuf_tensor(name, shape, dt))

        def sem(name):
            return ctx.enter_context(nc.semaphore(name))

        ident = sb("j_ident", [P, P])
        xs = sb("j_x", [P, NTOK, DIM])
        ss = sb("j_s", [P, TOKENS])
        sil = sb("j_silu", [P, 2, 512])
        prod = sb("j_prod", [P, 2, 512])
        res = sb("j_res", [P, NTOK, DIM])
        ps = [ctx.enter_context(nc.psum_tensor(f"j_ps{i}", [P, 512], F32)) for i in range(2)]
        loaded, x_loaded, silued, multiplied = sem("j_loaded"), sem("j_x_loaded"), sem("j_silued"), sem("j_multiplied")
        turned, summed, stored = sem("j_turned"), sem("j_summed"), sem("j_stored")
        groups = TOKENS // 512
        block = ctx.enter_context(nc.Block())

        def add(dve, g):
            dve.wait_ge(turned, g + 1)
            nc.vector.tensor_tensor(res[:, 4 * g:4 * g + 4, :], ps[g % 2][:].rearrange("p (n d) -> p n d", d=DIM),
                                    xs[:, 4 * g:4 * g + 4, :], ALU.add).then_inc(summed, 1)

        @block.sync
        def _(sp):
            sp.dma_start(ident[:], identity).then_inc(loaded, 16)
            sp.dma_start(ss[:], s_dram).then_inc(loaded, 16)
            sp.dma_start(xs[:], x.rearrange("b (n p) d -> p (b n) d", p=P)).then_inc(x_loaded, 16)
            o = out.rearrange("b (n p) d -> p (b n) d", p=P)
            for g in range(groups):
                sp.wait_ge(summed, g + 1)
                sp.dma_start(o[:, 4 * g:4 * g + 4, :], res[:, 4 * g:4 * g + 4, :]).then_inc(stored, 16)
            sp.wait_ge(stored, 16 * groups)

        @block.scalar
        def _(act):
            for g in range(groups):
                b, c = divmod(g, SEQ // 512)
                at = b * ROW + PAD + 512 * c
                if g >= 2:
                    act.wait_ge(multiplied, g - 1)
                nc.scalar.activation(sil[:, g % 2, :], xt[:, at:at + 512], ACT.Silu).then_inc(silued, 1)

        @block.vector
        def _(dve):
            dve.wait_ge(loaded, 32)
            dve.wait_ge(x_loaded, 16)
            for g in range(groups):
                dve.wait_ge(silued, g + 1)
                if g >= 2:
                    dve.wait_ge(turned, g - 1)
                nc.vector.tensor_tensor(prod[:, g % 2, :], sil[:, g % 2, :], ss[:, 512 * g:512 * (g + 1)],
                                        ALU.mult).then_inc(multiplied, 1)
                if g >= 1:
                    add(dve, g - 1)
            add(dve, groups - 1)

        @block.tensor
        def _(pe):
            pe.wait_ge(loaded, 32)
            for g in range(groups):
                pe.wait_ge(multiplied, g + 1)
                if g >= 2:
                    pe.wait_ge(summed, g - 1)
                for k in range(4):
                    last = nc.tensor.transpose(ps[g % 2][:, P * k:P * (k + 1)], prod[:, g % 2, P * k:P * (k + 1)], ident[:])
                last.then_inc(turned, 1)


def build(nc, d, s_dram, out):
    with nc.sbuf_tensor("xt", [P, 2 * BATCH * ROW], F32) as xt:
        phase_norm(nc, d["x"], xt, d["identity"])
        phase_mamba(nc, xt, d, s_dram)
        phase_layers(nc, xt, d)
        phase_join(nc, xt, d["x"], s_dram, d["identity"], out)


def shape_constants():
    f32 = np.float32
    half = np.arange(0, DH, 2, dtype=f32)
    inv_freq = f32(1.0) / f32(10000.0) ** (half / f32(DH))
    t = np.arange(SEQ, dtype=f32)
    freqs = t[:, None] * inv_freq[None, :]
    base = (half + f32(0.4 * DH)) / f32(1.4 * DH)
    power = (t - SEQ // 2) / f32(WIN // 2)
    scale = base[None, :] ** power[:, None]
    rows = np.arange(P) % 32
    sign = np.where(np.arange(P) % DH < DH // 2, -1.0, 1.0).astype(f32)[:, None]
    cos, sin, sc = np.cos(freqs).T[rows], np.sin(freqs).T[rows] * sign, scale.T[rows]
    tables = np.stack([cos * sc, sin * sc, cos * (f32(1.0) / sc), sin * (f32(1.0) / sc)], 1).astype(f32)
    tables = tables.reshape(P, 4, NT, TILE).transpose(0, 2, 1, 3).reshape(P, NT, 4 * TILE)
    tables = np.concatenate([tables, np.where(np.arange(NT) > 0, 1.0, 0.0).astype(f32)[None, :, None].repeat(P, 0)], 2).reshape(P, -1)
    q = (np.arange(P) % WIN)[:, None]
    key = np.arange(2 * WIN)[None, :]
    seen = np.where(key < WIN, key >= q, key - WIN <= q)
    one = np.where(seen, 0.0, MASKED)
    first = np.where(seen & (key >= WIN), 0.0, MASKED)
    bf16 = np.dtype("bfloat16")
    pick = np.zeros((32, 32, P), f32)
    pick[np.arange(32), np.arange(32), :] = 1.0
    ones_half = np.zeros((P, 2, WIN), f32)
    ones_half[:64, 0], ones_half[64:, 1] = 1.0, 1.0
    halves = np.zeros((P, 2), f32)
    halves[:64, 0], halves[64:, 1] = 1.0, 1.0
    small = np.ones((P, 2), f32)
    small[:, 0], small[:, 1] = EPS, LN_SHIFT / 2 * np.log(2.0)
    return {
        "tables": tables, "mask": np.tile(one, (1, NWIN)).astype(bf16),
        "mask0": np.concatenate([first] + [one] * (NT - 1), 1).astype(bf16),
        "identity": np.eye(P, dtype=f32), "identity_b": np.eye(P).astype(bf16), "pick": pick,
        "ones_half": ones_half, "halves": halves, "mean_w": np.full((P, P), 1.0 / DIM, f32), "small": small,
    }


def laid_out(a):
    def cols(v, n):
        return v.reshape(n, P).T

    f32 = np.float32
    swap = np.arange(DH).reshape(2, DH // 2)[::-1].reshape(-1)
    wqkv = a["L0_ffn_Wqkv"].astype(f32)
    qk = wqkv[:, :, :2 * INNER].reshape(DEPTH, DIM, 2, 8, 2, DH)
    qk = np.stack([qk, qk[..., swap]], 4).reshape(DEPTH, DIM, -1)
    vec = np.zeros((P, 32), f32)
    vec[:, 0:4] = cols(a["L0_attn_in_proj_b"], 4)
    vec[:, 4:6] = cols(a["L0_attn_conv_b"], 2)
    vec[:, 6:8] = cols(a["L0_attn_dt_proj_b"], 2)
    vec[:, 8:10] = cols(a["L0_attn_D_param"], 2)
    vec[:, 10] = a["L0_attn_out_proj_b"]
    vec[:, 12:20] = a["L0_attn_conv_w"].reshape(2, P, CONV).transpose(1, 0, 2).reshape(P, -1)
    par = np.zeros((P, DEPTH, NPAR), f32)
    for k, name in enumerate(("L0_ffn_q_scale", "L0_ffn_k_scale")):
        v = a[name].T
        par[:, :, 2 * k] = np.tile(v, (2, 1))
        par[:, :, 2 * k + 1] = np.tile(v[swap], (2, 1))
    par[:, :, LG], par[:, :, LB], par[:, :, B2] = a["L0_ffn_ln_g"].T, a["L0_ffn_ln_b"].T, a["L0_ffn_b2"].T
    for part, at in ((0, B1A), (1, B1G)):
        for c in range(3):
            m = P if c < 2 else FFR
            par[:m, :, at + c] = a["L0_ffn_b1"][:, FF * part + P * c:FF * part + P * c + m].T
    w2 = np.zeros((DEPTH, 3 * P, DIM), f32)
    w2[:, :FF] = a["L0_ffn_W2"]
    return {
        "x": a["L0_attn_hidden_states"],
        "w_in": a["L0_attn_in_proj_w"].T,
        "w_x": a["L0_attn_x_proj_w"].T.reshape(2, P, 40).transpose(1, 0, 2),
        "w_dt": a["L0_attn_dt_proj_w"].T,
        "w_out": a["L0_attn_out_proj_w"].T.reshape(2, P, DIM).transpose(1, 0, 2),
        "m_vec": vec,
        "alog": a["L0_attn_A_log"].reshape(2, P, STATE).transpose(1, 0, 2),
        "wqk": qk.transpose(1, 0, 2).reshape(P, -1),
        "wv": wqkv[:, :, 2 * INNER:].transpose(1, 0, 2).reshape(P, -1),
        "wo": a["L0_ffn_Wo"].reshape(DEPTH, 8, P, DIM).transpose(2, 0, 1, 3).reshape(P, -1),
        "w1": a["L0_ffn_W1"].transpose(1, 0, 2).reshape(P, -1),
        "w2": w2.reshape(DEPTH, 3, P, DIM).transpose(2, 0, 1, 3).reshape(P, -1),
        "par": par.reshape(P, -1),
    }


def kernel(**inputs):
    from concourse import bacc
    from concourse.bass_utils import run_bass_kernel_spmd

    nc = bacc.Bacc("TRN2", target_bir_lowering=False, num_devices=1)
    arrays = {k: np.ascontiguousarray(v) for k, v in
              {**laid_out({k: np.asarray(v) for k, v in inputs.items()}), **shape_constants()}.items()}
    d = {k: nc.dram_tensor(f"in_{k}", v.shape, mybir.dt.from_np(v.dtype), kind="ExternalInput").ap() for k, v in arrays.items()}
    s_dram = nc.dram_tensor("mamba_out", (P, TOKENS), F32, kind="Internal").ap()
    out = nc.dram_tensor("out", (BATCH, SEQ, DIM), F32, kind="ExternalOutput").ap()
    build(nc, d, s_dram, out)
    r = run_bass_kernel_spmd(nc, [{f"in_{k}": v for k, v in arrays.items()}], core_ids=[0])
    return r.results[0]["out"]
```

```python
from contextlib import ExitStack

import numpy as np

import concourse.bass as bass
from concourse import mybir

F32 = mybir.dt.float32
F32R = mybir.dt.float32r
BF16 = mybir.dt.bfloat16
ALU = mybir.AluOpType
ACT = mybir.ActivationFunctionType
AX_X = mybir.AxisListType.X

P = 128
BATCH, SEQ, DIM = 2, 2048, 128
TOKENS = BATCH * SEQ
NTOK = TOKENS // P
INNER_M = 256
STATE = 16
DT_RANK = 8
CONV = 4
CH = 512
NCH = SEQ // CH
CHUNKS = BATCH * NCH
DEPTH, HEADS, DH, WIN = 6, 16, 64, 32
INNER = HEADS * DH
FF = 341
FFR = FF - 2 * P
TILE = 256
NT = SEQ // TILE
NWIN = TILE // WIN
HALO = WIN
PAD = 64
ROW = PAD + SEQ
UNITS = 4
TAB = 4 * TILE
QK_SCALE = 8.0
EPS = 1e-5
NORM_FLOOR = 1e-12
LN_SHIFT = 20
MASKED = -1e24
LN_EXP = "natural_log_exp_and_others"
NPARQ = 4
LG, LB, B2, B1A, B1G = 0, 1, 2, 3, 6
NPAR = NPARQ + 9


def wait_alone(eng, sem, value, spare):
    eng.wait_ge(sem, value)
    eng.sem_inc(spare, 1)


def wait_from(eng, sem, value):
    if not isinstance(value, int) or value > 0:
        eng.wait_ge(sem, value)


def pos(w):
    return (w % 2) * 4 + w // 2


def phase_norm(nc, x, xt, identity):
    with ExitStack() as ctx:
        def sb(name, shape, dt=F32):
            return ctx.enter_context(nc.sbuf_tensor(name, shape, dt))

        def sem(name):
            return ctx.enter_context(nc.semaphore(name))

        xin = sb("ln_x", [P, NTOK, DIM])
        sq = sb("ln_sq", [P, NTOK, DIM])
        mean = sb("ln_mean", [P, NTOK])
        var = sb("ln_var", [P, NTOK])
        dev = sb("ln_dev", [P, NTOK])
        rstd = sb("ln_rstd", [P, NTOK])
        ps = [ctx.enter_context(nc.psum_tensor(f"ln_ps{i}", [P, 512], F32)) for i in range(2)]
        ident = sb("ln_ident", [P, P])
        loaded, zeroed, step, squared, rooted = (sem(n) for n in ("ln_loaded", "ln_zeroed", "ln_step", "ln_squared", "ln_rooted"))
        turned, copied = sem("ln_turned"), sem("ln_copied")
        groups = TOKENS // 512
        block = ctx.enter_context(nc.Block())

        @block.sync
        def _(sp):
            sp.dma_start(xin[:], x.rearrange("b (n p) d -> p (b n) d", p=P)).then_inc(loaded, 16)
            sp.dma_start(ident[:], identity).then_inc(loaded, 16)

        @block.gpsimd
        def _(pool):
            for b in range(2 * BATCH):
                nc.gpsimd.memset(xt[:, b * ROW:b * ROW + PAD], 0.0).then_inc(zeroed, 1)
            pool.wait_ge(zeroed, 2 * BATCH)

        @block.scalar
        def _(act):
            act.wait_ge(step, 2)
            nc.scalar.activation(sq[:], xin[:], ACT.Square).then_inc(squared, 1)
            act.wait_ge(step, 4)
            nc.scalar.activation(dev[:], var[:], ACT.Sqrt).then_inc(rooted, 1)

        @block.vector
        def _(dve):
            def bc(t):
                return t[:].unsqueeze(2).broadcast_to([P, NTOK, DIM])
            dve.wait_ge(loaded, 32)
            nc.vector.tensor_reduce(mean[:], xin[:], AX_X, ALU.add).then_inc(step, 1)
            dve.wait_ge(step, 1)
            nc.vector.tensor_scalar(rstd[:], mean[:], 1.0 / DIM, None, ALU.mult).then_inc(rooted, 1)
            dve.wait_ge(rooted, 1)
            nc.vector.tensor_tensor(xin[:], xin[:], bc(rstd), ALU.subtract).then_inc(step, 1)
            dve.wait_ge(squared, 1)
            nc.vector.tensor_reduce(mean[:], sq[:], AX_X, ALU.add).then_inc(step, 1)
            dve.wait_ge(step, 3)
            nc.vector.tensor_scalar(var[:], mean[:], 1.0 / DIM, EPS, ALU.mult, ALU.add).then_inc(step, 1)
            dve.wait_ge(rooted, 2)
            nc.vector.reciprocal(rstd[:], dev[:]).then_inc(step, 1)
            dve.wait_ge(step, 5)
            nc.vector.tensor_tensor(xin[:], xin[:], bc(rstd), ALU.mult).then_inc(step, 1)
            for g in range(groups):
                dve.wait_ge(turned, g + 1)
                b, c = divmod(g, SEQ // 512)
                at = b * ROW + PAD + 512 * c
                nc.vector.tensor_copy(xt[:, at:at + 512], ps[g % 2][:]).then_inc(copied, 1)

        @block.tensor
        def _(pe):
            pe.wait_ge(step, 6)
            for g in range(groups):
                if g >= 2:
                    pe.wait_ge(copied, g - 1)
                for k in range(4):
                    last = nc.tensor.transpose(ps[g % 2][:, P * k:P * (k + 1)], xin[:, 4 * g + k, :], ident[:])
                last.then_inc(turned, 1)


def phase_mamba(nc, xt, d, s_dram):
    H2 = INNER_M // P
    with ExitStack() as ctx:
        def sb(name, shape, dt=F32):
            return ctx.enter_context(nc.sbuf_tensor(name, shape, dt))

        def psum(name, shape):
            return ctx.enter_context(nc.psum_tensor(name, shape, F32))

        def sem(name):
            return ctx.enter_context(nc.semaphore(name))

        w_in = sb("w_in", [P, 2 * INNER_M])
        w_x = sb("w_x", [P, H2, DT_RANK + 4 * STATE])
        w_dt = sb("w_dt", [DT_RANK, INNER_M])
        w_out = sb("w_out", [P, H2, DIM])
        pick_raw = sb("pick_raw", [64, 32, P])
        pick = sb("pick", [64, 32, P], F32R)
        ident = sb("m_ident", [P, P])
        vec = sb("m_vec", [P, 32])
        alog = sb("alog", [P, H2, STATE])
        aneg = sb("aneg", [P, H2, STATE])
        aexp = sb("aexp", [P, H2, STATE])
        xi = sb("xi", [P, H2, CONV - 1 + CH])
        zs = sb("zs", [P, H2, CH])
        cv = [sb(f"cv{i}", [P, H2, CH]) for i in range(2)]
        xc = sb("xc", [P, H2, CH])
        dt = sb("dt", [P, H2, CH])
        dtx = sb("dtx", [P, H2, CH])
        t_a = sb("t_a", [P, H2, CH])
        t_e = sb("t_e", [P, H2, CH])
        t_u = sb("t_u", [P, H2, CH])
        t_l = sb("t_l", [P, H2, CH])
        t_i = sb("t_i", [P, H2, CH])
        t_m = sb("t_m", [P, H2, CH])
        lr = sb("lr", [DT_RANK, CH])
        bc = sb("bc", [64, CH], F32R)
        bsp = sb("bsp", [P, 2, CH])
        dA = sb("dA", [P, 2, H2, CH])
        dBu = sb("dBu", [P, 2, H2, CH])
        hs = sb("hs", [P, 2, H2, CH])
        hc = sb("hc", [P, 2, H2, CH])
        state = sb("state", [P, STATE, H2])
        yg = sb("yg", [P, H2, CH])
        y2 = sb("y2", [P, H2, CH])
        so = sb("so", [P, CH])
        ps_a = psum("ps_a", [P, H2, 512])
        ps_b = [psum(f"ps_b{i}", [P, 512]) for i in range(2)]
        ps_c = [psum(f"ps_c{i}", [P, 512]) for i in range(2)]
        ps_y = psum("ps_y", [P, H2, 512])

        loaded = sem("m_loaded")
        a_ready = sem("a_ready")
        px_full = sem("px_full")
        px_free = sem("px_free")
        tail_kept = sem("tail_kept")
        conv_step = sem("conv_step")
        xc_ready = sem("xc_ready")
        bc_rounded = sem("bc_rounded")
        bc_ready = sem("bc_ready")
        pick_ready = sem("pick_ready")
        sp_act = sem("sp_act")
        sp_dve = sem("sp_dve")
        dtx_ready = sem("dtx_ready")
        b_full, c_full = sem("b_full"), sem("c_full")
        b_copied = sem("b_copied")
        da_ready, dbu_ready = sem("da_ready"), sem("dbu_ready")
        scanned = sem("scanned")
        kept = sem("state_kept")
        hc_ready = sem("hc_ready")
        y_added = sem("y_added")
        y_step = sem("y_step")
        stored = sem("s_stored")
        so_ready = sem("so_ready")
        zeroed = sem("m_zeroed")
        spare = sem("m_spare")
        block = ctx.enter_context(nc.Block())

        NLOAD = 8

        @block.sync
        def _(sp):
            for dst, src in ((w_in, "w_in"), (w_x, "w_x"), (w_dt, "w_dt"), (w_out, "w_out"), (pick_raw, "pick"),
                             (ident, "identity"), (vec, "m_vec"), (alog, "alog")):
                sp.dma_start(dst[:], d[src]).then_inc(loaded, 16)
            def body(it):
                sp.wait_ge(so_ready, it + 1)
                sp.dma_start(s_dram[:, bass.ds(it * CH, CH)], so[:]).then_inc(stored, 16)

            body(0)
            with sp.Fori(1, CHUNKS) as it:
                body(it)
            sp.wait_ge(stored, 16 * BATCH * NCH)

        @block.tensor
        def _(pe):
            pe.wait_ge(loaded, 16 * NLOAD)
            pe.wait_ge(pick_ready, 1)
            def body(it):
                src = xt[:, bass.ds(it // NCH * ROW + it % NCH * CH + PAD, CH)]
                for use in range(2):
                    if use == 0:
                        wait_from(pe, so_ready, it)
                    else:
                        pe.wait_ge(px_free, it * 4 + 1)
                    for h in range(H2):
                        k = use * H2 + h
                        last = nc.tensor.matmul(ps_a[:, h, :], w_in[:, P * k:P * (k + 1)], src, start=True, stop=True)
                    last.then_inc(px_full, 1)
                pe.wait_ge(px_free, it * 4 + 2)
                pe.wait_ge(xc_ready, it + 1)
                for h in range(H2):
                    nc.tensor.matmul(ps_a[0:DT_RANK, 0, :], w_x[:, h, 0:DT_RANK], xc[:, h, :],
                                     start=(h == 0), stop=(h == H2 - 1))
                for h in range(H2):
                    last = nc.tensor.matmul(ps_a[0:64, 1, :], w_x[:, h, DT_RANK:], xc[:, h, :],
                                            start=(h == 0), stop=(h == H2 - 1))
                last.then_inc(px_full, 1)
                pe.wait_ge(px_free, it * 4 + 3)
                pe.wait_ge(bc_ready, it + 1)
                for h in range(H2):
                    last = nc.tensor.matmul(ps_a[:, h, :], w_dt[:, P * h:P * (h + 1)], lr[:], start=True, stop=True)
                last.then_inc(px_full, 1)

                def spread_b(n):
                    wait_from(pe, b_copied, it * STATE + max(n - 1, 0))
                    nc.tensor.matmul(ps_b[n % 2][:], pick[:, n, :], bc[:], start=True, stop=True).then_inc(b_full, 1)

                def spread_c(n):
                    wait_from(pe, hc_ready, it * STATE + max(n - 1, 0))
                    nc.tensor.matmul(ps_c[n % 2][:], pick[:, STATE + n, :], bc[:], start=True, stop=True).then_inc(c_full, 1)

                def add(n):
                    pe.wait_ge(hc_ready, it * STATE + n + 1)
                    if n == 0:
                        wait_from(pe, y_step, it * 2)
                    for h in range(H2):
                        last = nc.tensor.matmul(ps_y[:, h, :], ident[:], hc[:, n % 2, h, :],
                                                start=(n == 0), stop=(n == STATE - 1))
                    last.then_inc(y_added, 1)

                for n in range(2):
                    spread_b(n)
                    spread_c(n)
                for n in range(STATE):
                    if n + 2 < STATE:
                        spread_b(n + 2)
                    add(n)
                    if n + 2 < STATE:
                        spread_c(n + 2)
                pe.wait_ge(px_free, it * 4 + 4)
                pe.wait_ge(y_step, it * 2 + 2)
                for h in range(H2):
                    last = nc.tensor.matmul(ps_a[:, 0, :], w_out[:, h, :], y2[:, h, :],
                                            start=(h == 0), stop=(h == H2 - 1))
                last.then_inc(px_full, 1)

            body(0)
            with pe.Fori(1, CHUNKS) as it:
                body(it)

        @block.scalar
        def _(act):
            act.wait_ge(loaded, 16 * NLOAD)
            nc.scalar.activation(aexp[:], alog[:], ACT.Exp).then_inc(a_ready, 1)
            act.wait_ge(a_ready, 1)
            nc.scalar.mul(aneg[:], aexp[:], -1.0).then_inc(a_ready, 1)
            act.wait_ge(a_ready, 2)
            def body(it):
                act.wait_ge(px_full, it * 5 + 1)
                act.wait_ge(tail_kept, it + 1)
                for h in range(H2):
                    last = nc.scalar.activation(xi[:, h, CONV - 1:], ps_a[:, h, :], ACT.Identity, bias=vec[:, h:h + 1])
                last.then_inc(px_free, 1)
                act.wait_ge(px_full, it * 5 + 2)
                wait_from(act, y_step, it * 2)
                for h in range(H2):
                    last = nc.scalar.activation(zs[:, h, :], ps_a[:, h, :], ACT.Silu, bias=vec[:, 2 + h:3 + h])
                last.then_inc(px_free, 1)
                act.wait_ge(conv_step, (it + 1) * CONV * H2)
                for h in range(H2):
                    last = nc.scalar.activation(xc[:, h, :], cv[(CONV - 1) % 2][:, h, :], ACT.Silu, bias=vec[:, 4 + h:5 + h])
                last.then_inc(xc_ready, 1)
                act.wait_ge(px_full, it * 5 + 3)
                nc.scalar.copy(bc[:], ps_a[0:64, 1, :]).then_inc(bc_rounded, 1)
                nc.scalar.copy(lr[:], ps_a[0:DT_RANK, 0, :]).then_inc(px_free, 1)
                act.wait_ge(px_full, it * 5 + 4)
                wait_from(act, dtx_ready, it)
                for h in range(H2):
                    last = nc.scalar.activation(t_a[:, h, :], ps_a[:, h, :], ACT.Abs, bias=vec[:, 6 + h:7 + h])
                last.then_inc(sp_act, 1)
                nc.scalar.preload_act_table_set(LN_EXP)
                act.wait_ge(sp_act, it * 4 + 1)
                nc.scalar.activation(t_e[:], t_a[:], ACT.Exp, scale=-1.0).then_inc(sp_act, 1)
                act.wait_ge(sp_dve, it * 5 + 1)
                nc.scalar.activation(t_l[:], t_u[:], ACT.Ln).then_inc(sp_act, 1)
                act.wait_ge(sp_act, it * 4 + 3)
                nc.scalar.activation(t_i[:], t_l[:], ACT.Exp, scale=-1.0).then_inc(sp_act, 1)

                def decay(n):
                    wait_from(act, scanned, it * STATE + max(n - 1, 0))
                    for h in range(H2):
                        last = nc.scalar.activation(dA[:, n % 2, h, :], dt[:, h, :], ACT.Exp, scale=aneg[:, h, n:n + 1])
                    last.then_inc(da_ready, 1)

                def take_b(n):
                    act.wait_ge(b_full, it * STATE + n + 1)
                    wait_from(act, dbu_ready, it * STATE + max(n - 1, 0))
                    nc.scalar.copy(bsp[:, n % 2, :], ps_b[n % 2][:]).then_inc(b_copied, 1)

                act.wait_ge(sp_dve, it * 5 + 5)
                for n in range(STATE):
                    take_b(n)
                    decay(n)
                act.wait_ge(px_full, it * 5 + 5)
                wait_from(act, stored, it * 16)
                nc.scalar.activation(so[:], ps_a[:, 0, :], ACT.Identity, bias=vec[:, 10:11]).then_inc(so_ready, 1)

            body(0)
            with act.Fori(1, CHUNKS) as it:
                body(it)

        @block.gpsimd
        def _(pool):
            def body(it):
                pool.wait_ge(dtx_ready, it + 1)
                for n in range(STATE):
                    pool.wait_ge(b_copied, it * STATE + n + 1)
                    wait_from(pool, scanned, it * STATE + max(n - 1, 0))
                    nc.gpsimd.tensor_tensor(dBu[:, n % 2], dtx[:], bsp[:, n % 2, :].unsqueeze(1).broadcast_to([P, H2, CH]),
                                            ALU.mult).then_inc(dbu_ready, 1)

            body(0)
            with pool.Fori(1, CHUNKS) as it:
                body(it)

        @block.vector
        def _(dve):
            dve.wait_ge(loaded, 16 * NLOAD)
            nc.vector.tensor_copy(pick[:], pick_raw[:]).then_inc(pick_ready, 1)
            def start(b):
                wait_from(dve, kept, b * NCH * STATE)
                nc.vector.memset(state[:], 0.0).then_inc(zeroed, 1)
                nc.vector.memset(xi[:, :, CH:CH + CONV - 1], 0.0).then_inc(zeroed, 1)
                dve.wait_ge(zeroed, 2 * b + 2)

            def body(it):
                wait_from(dve, conv_step, it * CONV * H2)
                nc.vector.tensor_copy(xi[:, :, 0:CONV - 1], xi[:, :, CH:CH + CONV - 1]).then_inc(tail_kept, 1)
                dve.wait_ge(px_free, it * 4 + 1)
                for k in range(CONV):
                    if k:
                        dve.wait_ge(conv_step, it * CONV * H2 + k * H2)
                    else:
                        wait_from(dve, xc_ready, it)
                    for h in range(H2):
                        tap = vec[:, 12 + CONV * h + k:13 + CONV * h + k]
                        seen = xi[:, h, k:k + CH]
                        if k == 0:
                            i = nc.vector.tensor_scalar(cv[0][:, h, :], seen, tap, None, ALU.mult)
                        else:
                            i = nc.vector.scalar_tensor_tensor(out=cv[k % 2][:, h, :], in0=seen, scalar=tap,
                                                               in1=cv[(k - 1) % 2][:, h, :], op0=ALU.mult, op1=ALU.add)
                        i.then_inc(conv_step, 1)
                dve.wait_ge(bc_rounded, it + 1)
                nc.vector.tensor_tensor(bc[32:64], ps_a[32:64, 1, :], bc[32:64].bitcast(F32), ALU.subtract).then_inc(bc_ready, 1)
                dve.wait_ge(sp_act, it * 4 + 1)
                for h in range(H2):
                    i = nc.vector.tensor_scalar(t_m[:, h, :], ps_a[:, h, :], vec[:, 6 + h:7 + h], 0.0, ALU.add, ALU.max)
                i.then_inc(px_free, 1)
                dve.wait_ge(sp_act, it * 4 + 2)
                nc.vector.tensor_scalar(t_u[:], t_e[:], 1.0, None, ALU.add).then_inc(sp_dve, 1)
                dve.wait_ge(sp_dve, it * 5 + 1)
                nc.vector.scalar_tensor_tensor(out=t_e[:], in0=t_u[:], scalar=-1.0, in1=t_e[:], op0=ALU.add,
                                               op1=ALU.subtract).then_inc(sp_dve, 1)
                dve.wait_ge(sp_dve, it * 5 + 2)
                dve.wait_ge(sp_act, it * 4 + 4)
                nc.vector.tensor_tensor(t_e[:], t_e[:], t_i[:], ALU.mult).then_inc(sp_dve, 1)
                dve.wait_ge(sp_dve, it * 5 + 3)
                nc.vector.tensor_tensor(t_m[:], t_m[:], t_e[:], ALU.subtract).then_inc(sp_dve, 1)
                dve.wait_ge(sp_dve, it * 5 + 4)
                wait_from(dve, da_ready, it * STATE)
                nc.vector.tensor_tensor(dt[:], t_m[:], t_l[:], ALU.add).then_inc(sp_dve, 1)
                dve.wait_ge(sp_dve, it * 5 + 5)
                wait_from(dve, dbu_ready, it * STATE)
                nc.vector.tensor_tensor(dtx[:], dt[:], xc[:], ALU.mult).then_inc(dtx_ready, 1)
                for n in range(STATE):
                    dve.wait_ge(da_ready, it * STATE + n + 1)
                    dve.wait_ge(dbu_ready, it * STATE + n + 1)
                    wait_from(dve, hc_ready, it * STATE + max(n - 1, 0))
                    wait_from(dve, kept, it * STATE + n)
                    for h in range(H2):
                        i = nc.vector.tensor_tensor_scan(hs[:, n % 2, h, :], dA[:, n % 2, h, :], dBu[:, n % 2, h, :],
                                                         state[:, n, h:h + 1], ALU.mult, ALU.add)
                    i.then_inc(scanned, 1)
                    dve.wait_ge(scanned, it * STATE + n + 1)
                    nc.vector.tensor_copy(state[:, n, :], hs[:, n % 2, :, CH - 1]).then_inc(kept, 1)
                    dve.wait_ge(c_full, it * STATE + n + 1)
                    wait_from(dve, y_added, it * STATE + max(n - 1, 0))
                    nc.vector.tensor_tensor(hc[:, n % 2], hs[:, n % 2], ps_c[n % 2][:].unsqueeze(1).broadcast_to([P, H2, CH]),
                                            ALU.mult).then_inc(hc_ready, 1)
                dve.wait_ge(y_added, (it + 1) * STATE)
                for h in range(H2):
                    i = nc.vector.scalar_tensor_tensor(out=yg[:, h, :], in0=xc[:, h, :], scalar=vec[:, 8 + h:9 + h],
                                                       in1=ps_y[:, h, :], op0=ALU.mult, op1=ALU.add)
                i.then_inc(y_step, 1)
                dve.wait_ge(y_step, it * 2 + 1)
                wait_from(dve, px_full, it * 5)
                nc.vector.tensor_tensor(y2[:], yg[:], zs[:], ALU.mult).then_inc(y_step, 1)

            start(0)
            body(0)
            with dve.Fori(1, NCH) as it:
                body(it)
            start(1)
            with dve.Fori(NCH, CHUNKS) as it:
                body(it)

def jobs_of_a_turn():
    order = []
    for s in range(UNITS):
        order += [("qk", s, 0), ("qk", s, 1), ("norm", s - 1)]
        if s == 2:
            order.append(("mean", -1))
        order.append(("qk", s, 2))
        if s == 3:
            order += [("hidden", -1, 0), ("hidden", -1, 1)]
        order.append(("qk", s, 3))
        if s == 1:
            order += [("v", 0, i) for i in range(2)] + [("wo", -1, b) for b in range(BATCH)]
        if s == 2:
            order.append(("var", -1))
        if s == 3:
            order += [("hidden", -1, 2)] + [("v", 1, i) for i in range(2)] + [("out", -1)]
    return order


JOBS = jobs_of_a_turn()
assert len(JOBS) % 2 == 0
PER_SLOT = len(JOBS) // 2
TURNS = DEPTH * NT


def late(job):
    return job[1] < 0


LATE = [sum(late(j) for j in JOBS[s::2]) for s in range(2)]


def has_new(it):
    return not isinstance(it, int) or it < TURNS


def has_old(it):
    return not isinstance(it, int) or it > 0


def has(it, k):
    return has_new(it) if k >= 0 else has_old(it)


def slot_of(job):
    return JOBS.index(job) % 2


def jobs_before(it, job):
    n = JOBS.index(job)
    slot, before = n % 2, JOBS[n % 2:n:2]
    if isinstance(it, int) and it == 0:
        return sum(not late(j) for j in before)
    if isinstance(it, int) and it == TURNS:
        return TURNS * PER_SLOT - LATE[slot] + sum(late(j) for j in before)
    return it * PER_SLOT + (len(before) - LATE[slot])


def phase_layers(nc, xt, d):
    with ExitStack() as ctx:
        def sb(name, shape, dt=F32):
            return ctx.enter_context(nc.sbuf_tensor(name, shape, dt))

        def sem(name):
            return ctx.enter_context(nc.semaphore(name))

        wqk = sb("wqk", [P, 2, 8, 2, P])
        wv = sb("wv", [P, INNER])
        wo = sb("wo", [P, 8, DIM])
        w1 = sb("w1", [P, 2 * FF])
        w2 = sb("w2", [P, 3, DIM])
        parq = sb("parq", [P, NPARQ])
        par = sb("par", [P, NPAR - NPARQ])
        tabs = sb("tabs", [P, 2 * TAB])
        flags = sb("flags", [P, NT])
        flag = sb("flag", [P, 1])
        mask = sb("mask", [P, 512], BF16)
        mask0 = sb("mask0", [P, NT * 2 * WIN], BF16)
        ident_b = sb("ident_b", [P, P], BF16)
        ident = sb("l_ident", [P, P])
        ones_half = sb("ones_half", [P, 2, WIN])
        halves = sb("halves", [P, 2])
        mean_w = sb("mean_w", [P, P])
        small = sb("small", [P, 2])
        xin = sb("xin", [P, BATCH, HALO + TILE])
        t_qk = sb("t_qk", [P, 2, 2, 2, TILE])
        qr = sb("qr", [P, 2, 4, TILE])
        kr = sb("kr", [P, UNITS, 4, HALO + TILE])
        sqs = sb("sqs", [P, 2, 2, 4, TILE])
        kss = sb("kss", [P, 2, 512])
        qss = sb("qss", [P, 2, 2 * NWIN])
        kinv = sb("kinv", [P, UNITS, 2, HALO + TILE])
        qinv = sb("qinv", [P, 2, 2 * NWIN])
        pr = sb("pr", [P, 2, 2, 512])
        smax = sb("smax", [P, 2, 2 * NWIN])
        ssum = sb("ssum", [P, 2, 2 * NWIN])
        sinv = sb("sinv", [P, 2, 2 * NWIN])
        prt = sb("prt", [P, 2, 4, 4, 2, WIN])
        vals = sb("vals", [P, 4, INNER])
        vhalo = sb("vhalo", [P, INNER])
        ot = sb("ot", [P, BATCH, 2, 4, TILE])
        x1 = sb("x1", [P, BATCH, 1 + TILE])
        xf = sb("xf", [P, BATCH, TILE])
        xsq = sb("xsq", [P, 512])
        rstd = sb("l_rstd", [P, 512])
        xn = sb("xn", [P, 512])
        gate = sb("gate", [P, 3, 512])
        ring = [ctx.enter_context(nc.psum_tensor(f"ring{i}", [P, 2, 512], F32)) for i in range(2)]
        ps_s = ctx.enter_context(nc.psum_tensor("ps_s", [P, 2, 512], F32))
        ps_p = ctx.enter_context(nc.psum_tensor("ps_p", [P, 2, 512], F32))

        consts = sem("consts")
        cleared = sem("cleared")
        wqk_in, wv_in, wo_in, wf_in = sem("wqk_in"), sem("wv_in"), sem("wo_in"), sem("wf_in")
        tab_in = sem("tab_in")
        flag_ready = sem("flag_ready")
        xin_ready = sem("xin_ready")
        full = [sem(f"slot{i}_full") for i in range(2)]
        free = [sem(f"slot{i}_free") for i in range(2)]
        squared = sem("l_squared")
        added = sem("added")
        halo_moved = sem("halo_moved")
        inv_step = sem("inv_step")
        inv_ready = sem("inv_ready")
        scores_done = sem("scores_done")
        sm_step = sem("sm_step")
        q_scaled = sem("q_scaled")
        exp_done = sem("exp_done")
        sum_step = sem("sum_step")
        p_normed = sem("p_normed")
        turned = sem("l_turned")
        turned_read = sem("turned_read")
        pv_done = sem("pv_done")
        ot_ready = sem("ot_ready")
        x1_step = sem("x1_step")
        ff_dve = sem("ff_dve")
        ff_act = sem("ff_act")
        gated = sem("gated")
        vals_kept = sem("vals_kept")
        vals_in = sem("vals_in")
        spare = {e: sem(f"spare_{e}") for e in ("sp", "pe", "pool", "dve")}
        block = ctx.enter_context(nc.Block())
        NCONST = 9

        def wait_full(eng, it, job):
            eng.wait_ge(full[slot_of(job)], jobs_before(it, job) + 1)

        def wait_taken(eng, it, job):
            eng.wait_ge(free[slot_of(job)], jobs_before(it, job) + 1)

        def wait_free(pe, it, job):
            wait_from(pe, free[slot_of(job)], jobs_before(it, job))

        OUT_SLOT = slot_of(("out", -1))

        def wait_turns(eng, it):
            wait_from(eng, free[OUT_SLOT], it * PER_SLOT - LATE[OUT_SLOT])

        def unit(k):
            return (k % UNITS) // 2, k % 2

        @block.sync
        def _(sp):
            sp.dma_start(tabs[:, 0:TAB], d["tables"][:, 0:TAB]).then_inc(tab_in, 16)
            for dst, src in ((mask, "mask"), (mask0, "mask0"), (ident_b, "identity_b"), (ident, "identity"), (flags, "flags"),
                             (ones_half, "ones_half"), (halves, "halves"), (mean_w, "mean_w"), (small, "small")):
                sp.dma_start(dst[:], d[src]).then_inc(consts, 16)

            def next_tables(l, i):
                it = l * NT + i
                wait_alone(sp, tab_in, it * 16 + 16, spare["sp"])
                wait_from(sp, added, it * 16)
                sp.dma_start(tabs[:, bass.ds((it + 1) % 2 * TAB, TAB)],
                             d["tables"][:, bass.ds((i + 1) % NT * TAB, TAB)]).then_inc(tab_in, 16)

            def load_layer(l):
                wait_from(sp, added, l * NT * 16)
                sp.dma_start(wqk[:], d["wqk"][:, bass.ds(l * 4096, 4096)]).then_inc(wqk_in, 16)
                sp.dma_start(parq[:], d["parq"][:, bass.ds(l * NPARQ, NPARQ)]).then_inc(wqk_in, 16)
                if not isinstance(l, int):
                    wait_turns(sp, l * NT)
                sp.dma_start(wv[:], d["wv"][:, bass.ds(l * INNER, INNER)]).then_inc(wv_in, 16)
                next_tables(l, 0)
                if not isinstance(l, int):
                    wait_turns(sp, l * NT + 1)
                sp.dma_start(wo[:], d["wo"][:, bass.ds(l * 8 * DIM, 8 * DIM)]).then_inc(wo_in, 16)
                sp.dma_start(w1[:], d["w1"][:, bass.ds(l * 2 * FF, 2 * FF)]).then_inc(wf_in, 16)
                sp.dma_start(w2[:], d["w2"][:, bass.ds(l * 3 * DIM, 3 * DIM)]).then_inc(wf_in, 16)
                sp.dma_start(par[:], d["par"][:, bass.ds(l * (NPAR - NPARQ), NPAR - NPARQ)]).then_inc(wf_in, 16)
                with sp.Fori(1, NT) as i:
                    next_tables(l, i)

            load_layer(0)
            with sp.Fori(1, DEPTH) as l:
                load_layer(l)
            sp.wait_ge(tab_in, 16 * (TURNS + 1))

        @block.tensor
        def _(pe):
            def qk(it, s, j):
                b, o = unit(s)
                if s % 2 + j == 0:
                    pe.wait_ge(xin_ready, it * 4 + 2 * b + 2)
                wait_free(pe, it, ("qk", s, j))
                ps = ring[slot_of(("qk", s, j))]
                for part in range(2):
                    for c in range(2):
                        last = nc.tensor.matmul(ps[:, part, TILE * c:TILE * (c + 1)], wqk[:, j // 2, 4 * o + 2 * (j % 2) + c, part, :],
                                                xin[:, b, HALO:], start=True, stop=True)
                last.then_inc(full[slot_of(("qk", s, j))], 1)

            def norm(it, k):
                job = ("norm", k)
                wait_free(pe, it, job)
                slot = slot_of(job)
                ps = ring[slot]
                pe.wait_ge(squared, (it * UNITS + k) * 4 + 4)
                for c in range(4):
                    for half in range(2):
                        nc.tensor.matmul(ps[32 * c:32 * c + 32, 0, TILE * half:TILE * (half + 1)], ones_half[:, half, :],
                                         sqs[:, k % 2, 1, c, :], start=True, stop=True)
                for c in range(4):
                    for w in range(NWIN):
                        p = pos(w)
                        last = nc.tensor.matmul(ps[32 * c:32 * c + 32, 1, 2 * p:2 * p + 2],
                                                sqs[:, k % 2, 0, c, WIN * w:WIN * (w + 1)], halves[:], start=True, stop=True)
                last.then_inc(full[slot], 1)

            def scores(it, k):
                n = it * UNITS + k
                i = (it + (NT - 1 if k < 0 else 0)) % NT
                wait_from(pe, sm_step, n * 4 - 2)
                pe.wait_ge(added, n * 4 + 4)
                for half in range(2):
                    nc.tensor.matmul(ps_s[:, half, 2 * WIN:], ident_b[:], mask[:, 2 * WIN:], start=True, stop=False,
                                     skip_group_check=True)
                    nc.tensor.matmul(ps_s[:, half, 0:2 * WIN], ident_b[:], mask0[:, bass.ds(i * 2 * WIN, 2 * WIN)], start=False, stop=False,
                                     skip_group_check=True)
                for c in range(4):
                    for w in range(NWIN):
                        for half in range(2):
                            r = slice(64 * half, 64 * half + 64)
                            last = nc.tensor.matmul(ps_s[32 * c:32 * c + 32, half, 64 * pos(w):64 * pos(w) + 64],
                                                    qr[r, k % 2, c, WIN * w:WIN * (w + 1)],
                                                    kr[r, k % UNITS, c, WIN * w:WIN * (w + 2)], start=False, stop=True,
                                                    skip_group_check=True)
                last.then_inc(scores_done, 1)

            def value(it, b):
                for i in range(2):
                    job = ("v", b, i)
                    wait_free(pe, it, job)
                    slot = slot_of(job)
                    first = HALO + P * i
                    for n in range(2):
                        last = nc.tensor.matmul(ring[slot][:, n, :], xin[:, b, first:first + P], wv[:, 512 * n:512 * (n + 1)],
                                                start=True, stop=True)
                    last.then_inc(full[slot], 1)

            def turn(it, s):
                n = it * UNITS + s
                pe.wait_ge(p_normed, n + 1)
                wait_from(pe, ot_ready, n)
                for half in range(2):
                    for k in range(4):
                        last = nc.tensor.transpose(ps_p[:, half, P * k:P * (k + 1)], pr[:, s % 2, half, P * k:P * (k + 1)], ident[:])
                last.then_inc(turned, 1)

            def weigh(it, s):
                b, o = unit(s)
                pe.wait_ge(vals_in, 48 * (it * BATCH + s // 2 + 1))
                wait_alone(pe, turned_read, it * UNITS + s + 1, spare["pe"])
                for c in range(4):
                    for k in range(4):
                        for half in range(2):
                            head = 8 * o + 2 * c + half
                            at = TILE * (c % 2) + 2 * WIN * k
                            last = nc.tensor.matmul(ps_p[64 * half:64 * half + 64, c // 2, at:at + 2 * WIN],
                                                    vals[:, k, DH * head:DH * (head + 1)],
                                                    prt[:, half, k, c].rearrange("p l q -> p (l q)"), start=True, stop=True)
                last.then_inc(pv_done, 1)

            def project(it, b):
                job = ("wo", -1, b)
                wait_free(pe, it, job)
                slot = slot_of(job)
                pe.wait_ge(ot_ready, (it - 1) * UNITS + 2 * b + 2)
                for o in range(2):
                    for c in range(4):
                        last = nc.tensor.matmul(ring[slot][:, 0, 0:TILE], wo[:, 4 * o + c, :], ot[:, b, o, c, :],
                                                start=(o + c == 0), stop=(o + c == 4))
                last.then_inc(full[slot], 1)

            def average(it, name):
                job = (name, -1)
                wait_free(pe, it, job)
                slot = slot_of(job)
                if name == "mean":
                    pe.wait_ge(ff_dve, (it - 1) * 4 + 2)
                else:
                    pe.wait_ge(ff_act, (it - 1) * 2 + 1)
                nc.tensor.matmul(ring[slot][:, 0, :], mean_w[:], xf[:] if name == "mean" else xsq[:],
                                 start=True, stop=True).then_inc(full[slot], 1)

            def hidden(it, c):
                job = ("hidden", -1, c)
                wait_free(pe, it, job)
                slot = slot_of(job)
                if c == 0:
                    pe.wait_ge(ff_dve, (it - 1) * 4 + 4)
                m = P if c < 2 else FFR
                for part in range(2):
                    last = nc.tensor.matmul(ring[slot][0:m, part, :], w1[:, FF * part + P * c:FF * part + P * c + m],
                                            xn[:], start=True, stop=True)
                last.then_inc(full[slot], 1)

            def hidden_out(it):
                job = ("out", -1)
                wait_free(pe, it, job)
                slot = slot_of(job)
                wait_taken(pe, it, ("hidden", -1, 2))
                for c in range(3):
                    m = P if c < 2 else FFR
                    last = nc.tensor.matmul(ring[slot][:, 0, :], w2[0:m, c, :], gate[0:m, c, :], start=(c == 0), stop=(c == 2))
                last.then_inc(full[slot], 1)

            def body(it):
                if has_new(it):
                    wait_alone(pe, wqk_in, 32 * (it // NT) + 32, spare["pe"])
                for s in range(UNITS):
                    if has_new(it):
                        qk(it, s, 0)
                        qk(it, s, 1)
                    if has(it, s - 1):
                        norm(it, s - 1)
                    if s == 2 and has_old(it):
                        average(it, "mean")
                    if has_new(it):
                        qk(it, s, 2)
                    if has(it, s - 1):
                        scores(it, s - 1)
                    if s == 3 and has_old(it):
                        wait_alone(pe, wf_in, 48 * ((it - 1) // NT) + 48, spare["pe"])
                        hidden(it, 0)
                    if has(it, s - 2):
                        turn(it, s - 2)
                    if s == 3 and has_old(it):
                        hidden(it, 1)
                    if has_new(it):
                        qk(it, s, 3)
                    if has(it, s - 2):
                        weigh(it, s - 2)
                    if s == 2 and has_old(it):
                        average(it, "var")
                    if s == 3 and has_old(it):
                        hidden(it, 2)
                    if s in (1, 3) and has_new(it):
                        if s == 1:
                            wait_alone(pe, wv_in, 16 * (it // NT) + 16, spare["pe"])
                        value(it, s // 2)
                    if s == 1 and has_old(it):
                        wait_alone(pe, wo_in, 16 * ((it - 1) // NT) + 16, spare["pe"])
                        for b in range(BATCH):
                            project(it, b)
                    if s == 3 and has_old(it):
                        hidden_out(it)

            pe.wait_ge(consts, 16 * NCONST)
            pe.wait_ge(cleared, 5)
            body(0)
            with pe.Fori(1, TURNS) as it:
                body(it)
            body(TURNS)

        @block.scalar
        def _(act):
            def square(it, s, j):
                wait_full(act, it, ("qk", s, j))
                ps = ring[slot_of(("qk", s, j))]
                nc.scalar.activation(sqs[:, s % 2, j // 2, 2 * (j % 2):2 * (j % 2) + 2, :], ps[:, 0, :], ACT.Square).then_inc(squared, 1)

            def invert(it, k):
                n, p = it * UNITS + k, k % 2
                wait_taken(act, it, ("norm", k))
                nc.scalar.activation(kss[:, p, :], kss[:, p, :], ACT.Ln, scale=float(2 ** LN_SHIFT)).then_inc(inv_step, 1)
                nc.scalar.activation(qss[:, p, :], qss[:, p, :], ACT.Ln, scale=float(2 ** LN_SHIFT)).then_inc(inv_step, 1)
                act.wait_ge(inv_step, n * 2 + 2)
                act.wait_ge(halo_moved, n * 2 + 2)
                wait_from(act, q_scaled, n - 1)
                nc.scalar.activation(kinv[:, k % UNITS, :, HALO:], kss[:, p, :], ACT.Exp, scale=-0.5, bias=small[:, 1:2]).then_inc(inv_ready, 1)
                nc.scalar.activation(qinv[:, p, :], qss[:, p, :], ACT.Exp, scale=-0.5, bias=small[:, 1:2]).then_inc(inv_ready, 1)

            def exps(it, k):
                act.wait_ge(q_scaled, it * UNITS + k + 1)
                nc.scalar.activation(pr[:, k % 2], pr[:, k % 2], ACT.Exp, scale=QK_SCALE).then_inc(exp_done, 1)

            def values(it, b):
                for i in range(2):
                    wait_full(act, it, ("v", b, i))
                    if i == 0:
                        wait_from(act, pv_done, it * UNITS + 2 * b)
                        wait_from(act, vals_kept, 16 * (it * BATCH + b))
                    slot = slot_of(("v", b, i))
                    nc.scalar.copy(vals[:, 2 + i, :], ring[slot][:]).then_inc(free[slot], 1)
                wait_taken(act, it, ("v", b, 0))
                wait_taken(act, it, ("v", b, 1))
                nc.scalar.dma_start(vals[WIN:, 0:2, :], vals[0:P - WIN, 2:4, :]).then_inc(vals_in, 16)
                nc.scalar.dma_start(vals[0:WIN, 1, :], vals[P - WIN:, 2, :]).then_inc(vals_in, 16)
                nc.scalar.dma_start(vals[0:WIN, 0, :], vhalo[WIN * b:WIN * (b + 1), :]).then_inc(vals_in, 16)

            def keep_values(it, b):
                g = it * BATCH + b
                act.wait_ge(vals_in, 48 * g + 48)
                nc.scalar.dma_start(vhalo[WIN * b:WIN * (b + 1), :], vals[P - WIN:, 3, :]).then_inc(vals_kept, 16)

            def take_turned(it, k):
                n = it * UNITS + k
                act.wait_ge(turned, n + 1)
                wait_from(act, pv_done, n)
                for lower in range(2):
                    r = slice(64 * lower, 64 * lower + 64)
                    last = nc.scalar.copy(prt[r, :, :, :, lower].rearrange("p h k c q -> p (h k c) q"),
                                          ps_p[r].rearrange("p h (m q) -> p (h m) q", q=WIN))
                last.then_inc(turned_read, 1)

            def take_out(it, k):
                b, o = unit(k)
                act.wait_ge(pv_done, it * UNITS + k + 1)
                nc.scalar.copy(ot[:, b, o].rearrange("p c t -> p (c t)"), ps_p[:].rearrange("p a t -> p (a t)")).then_inc(ot_ready, 1)

            def square_deviation(it):
                wait_taken(act, it, ("mean", -1))
                nc.scalar.activation(xsq[:], xf[:].rearrange("p b t -> p (b t)"), ACT.Square).then_inc(ff_act, 1)

            def invert_deviation(it):
                wait_full(act, it, ("var", -1))
                slot = slot_of(("var", -1))
                nc.scalar.activation(rstd[:], ring[slot][:, 0, :], ACT.Ln, bias=small[:, 0:1]).then_inc(free[slot], 1)
                wait_taken(act, it, ("var", -1))
                nc.scalar.activation(rstd[:], rstd[:], ACT.Exp, scale=-0.5).then_inc(ff_act, 1)

            def open_gate(it, c):
                m = P if c < 2 else FFR
                wait_full(act, it, ("hidden", -1, c))
                nc.scalar.activation(gate[0:m, c, :], ring[slot_of(("hidden", -1, c))][0:m, 1, :], ACT.Gelu,
                                     bias=par[0:m, B1G + c:B1G + c + 1]).then_inc(gated, 1)

            def body(it):
                for s in range(UNITS):
                    if has_new(it):
                        square(it, s, 0)
                        square(it, s, 1)
                    if has(it, s - 2):
                        exps(it, s - 2)
                    if s == 0 and has_new(it) and has_old(it):
                        keep_values(it - 1, 1)
                    if s == 2 and has_new(it):
                        keep_values(it, 0)
                    if has(it, s - 1):
                        invert(it, s - 1)
                    if s == 3 and has_old(it):
                        nc.scalar.preload_act_table(ACT.Gelu)
                    if has_new(it):
                        square(it, s, 2)
                    if has(it, s - 2):
                        take_turned(it, s - 2)
                    if s == 2 and has_old(it):
                        square_deviation(it)
                    if s == 3 and has_old(it):
                        open_gate(it, 0)
                        open_gate(it, 1)
                    if has_new(it):
                        square(it, s, 3)
                    if has(it, s - 2):
                        take_out(it, s - 2)
                    if s == 2 and has_old(it):
                        invert_deviation(it)
                    if s == 3 and has_old(it):
                        open_gate(it, 2)
                        nc.scalar.preload_act_table_set(LN_EXP)
                    if s in (1, 3) and has_new(it):
                        values(it, s // 2)

            act.wait_ge(cleared, 5)
            act.wait_ge(consts, 16 * NCONST)
            nc.scalar.preload_act_table_set(LN_EXP)
            body(0)
            with act.Fori(1, TURNS) as it:
                body(it)
            body(TURNS)

        @block.gpsimd
        def _(pool):
            for t in (kr, kinv):
                nc.gpsimd.memset(t[:], 1.0).then_inc(cleared, 1)
            for t in (x1, prt, vhalo):
                nc.gpsimd.memset(t[:], 0.0).then_inc(cleared, 1)
            pool.wait_ge(cleared, 5)

            def keep_halo(it, s):
                n = it * UNITS + s
                if has_old(it):
                    wait_alone(pool, scores_done, n - UNITS + 1, spare["pool"])
                nc.gpsimd.tensor_scalar(kr[:, s, :, 0:HALO], kr[:, s, :, TILE:], flag[:], 1.0, ALU.mult, ALU.mult).then_inc(halo_moved, 1)
                if has_old(it):
                    wait_alone(pool, sm_step, (n - UNITS) * 4 + 4, spare["pool"])
                nc.gpsimd.tensor_copy(kinv[:, s, :, 0:HALO], kinv[:, s, :, TILE:]).then_inc(halo_moved, 1)

            def join(it, s, j):
                n = it * UNITS + s
                if j == 0:
                    wait_from(pool, scores_done, n - 1)
                if j == 2:
                    pool.wait_ge(halo_moved, n * 2 + 2)
                wait_taken(pool, it, ("qk", s, j))
                c = 2 * (j % 2)
                dst = qr[:, s % 2, c:c + 2, :] if j < 2 else kr[:, s, c:c + 2, HALO:]
                nc.gpsimd.tensor_tensor(dst, t_qk[:, j % 2, 0], t_qk[:, j % 2, 1], ALU.add).then_inc(added, 1)

            def scale_q(it, k):
                n = it * UNITS + k
                pool.wait_ge(sm_step, n * 4 + 4)
                pool.wait_ge(inv_ready, n * 2 + 2)
                q = qinv[:, k % 2, :].rearrange("p (w h) -> p h w", h=2)
                for half in range(2):
                    v = pr[:, k % 2, half].rearrange("p (w k) -> p w k", k=2 * WIN)
                    last = nc.gpsimd.tensor_tensor(v, v, q[:, half, :].unsqueeze(2).broadcast_to([P, NWIN, 2 * WIN]), ALU.mult)
                last.then_inc(q_scaled, 1)

            def normalise(it, k):
                pool.wait_ge(sum_step, (it * UNITS + k) * 2 + 2)
                v = pr[:, k % 2].rearrange("p h (w k) -> p (h w) k", k=2 * WIN)
                nc.gpsimd.tensor_tensor(v, v, sinv[:, k % 2, :].unsqueeze(2).broadcast_to([P, 2 * NWIN, 2 * WIN]),
                                        ALU.mult).then_inc(p_normed, 1)

            def body(it):
                for s in range(UNITS):
                    if has_new(it):
                        join(it, s, 0)
                        join(it, s, 1)
                    if has(it, s - 2):
                        normalise(it, s - 2)
                    if has_new(it):
                        if s == 0:
                            wait_alone(pool, flag_ready, it + 1, spare["pool"])
                        keep_halo(it, s)
                        join(it, s, 2)
                        join(it, s, 3)
                    if has(it, s - 1):
                        scale_q(it, s - 1)

            body(0)
            with pool.Fori(1, TURNS) as it:
                body(it)
            body(TURNS)

        @block.vector
        def _(dve):
            def shift_in(it, b):
                l, i = it // NT, it % NT
                for lower in range(2):
                    r = slice(64 * lower, 64 * lower + 64)
                    col = (l % 2) * (BATCH * ROW) + b * ROW + PAD - HALO - lower + i * TILE
                    nc.vector.tensor_copy(xin[r, b, :], xt[r, bass.ds(col, HALO + TILE)]).then_inc(xin_ready, 1)

            def set_flag(it):
                wait_from(dve, halo_moved, it * UNITS * 2)
                if has_old(it):
                    dve.wait_ge(x1_step, (it - 1) * 2 + 2)
                nc.vector.tensor_copy(flag[:], flags[:, bass.ds(it % NT, 1)]).then_inc(flag_ready, 1)

            def token_before(it):
                for b in range(BATCH):
                    nc.vector.tensor_scalar(x1[:, b, 0:1], x1[:, b, TILE:TILE + 1], flag[:], None, ALU.mult).then_inc(x1_step, 1)

            def rotate(it, s, j):
                job = ("qk", s, j)
                ps = ring[slot_of(job)]
                kq = j // 2
                wait_full(dve, it, job)
                g = it * 16 + 4 * s + j
                wait_from(dve, added, g - 1)
                for part in (1, 0):
                    if part == 0:
                        dve.wait_ge(squared, g + 1)
                    t = nc.vector.scalar_tensor_tensor(
                        out=t_qk[:, j % 2, part], in0=ps[:, part, :].rearrange("p (c t) -> p c t", c=2),
                        scalar=parq[:, 2 * kq + part:2 * kq + part + 1],
                        in1=tabs[:, bass.ds(it % 2 * TAB + (2 * kq + part) * TILE, TILE)].unsqueeze(1).broadcast_to([P, 2, TILE]),
                        op0=ALU.mult, op1=ALU.mult)
                    if part == 0:
                        t.then_inc(free[slot_of(job)], 1)

            def read_norms(it, k):
                job = ("norm", k)
                wait_full(dve, it, job)
                wait_from(dve, inv_ready, (it * UNITS + k - 1) * 2)
                slot = slot_of(job)
                nc.vector.tensor_scalar(qss[:, k % 2, :], ring[slot][:, 1, 0:2 * NWIN], NORM_FLOOR ** 2, None, ALU.max)
                nc.vector.tensor_scalar(kss[:, k % 2, :], ring[slot][:, 0, :], NORM_FLOOR ** 2, None,
                                        ALU.max).then_inc(free[slot], 1)

            def softmax_top(it, s):
                n = it * UNITS + s
                dve.wait_ge(scores_done, n + 1)
                dve.wait_ge(inv_ready, n * 2 + 1)
                wait_from(dve, turned, n - 1)
                for half in range(2):
                    kv = kinv[:, s % UNITS, half, :]
                    for c in range(2):
                        keys = bass.AP(kv.tensor, kv.offset + WIN * c, [kv.ap[0], [2 * WIN, 4], [1, 2 * WIN]])
                        cols = slice(4 * 2 * WIN * c, 4 * 2 * WIN * (c + 1))
                        last = nc.vector.tensor_tensor(pr[:, s % 2, half, cols].rearrange("p (w k) -> p w k", k=2 * WIN),
                                                       ps_s[:, half, cols].rearrange("p (w k) -> p w k", k=2 * WIN),
                                                       keys, ALU.mult)
                    last.then_inc(sm_step, 1)
                v = pr[:, s % 2].rearrange("p h (w k) -> p (h w) k", k=2 * WIN)
                dve.wait_ge(sm_step, n * 4 + 2)
                nc.vector.tensor_reduce(smax[:, s % 2, :], v, AX_X, ALU.max).then_inc(sm_step, 1)
                dve.wait_ge(sm_step, n * 4 + 3)
                nc.vector.tensor_tensor(v, v, smax[:, s % 2, :].unsqueeze(2).broadcast_to([P, 2 * NWIN, 2 * WIN]),
                                        ALU.subtract).then_inc(sm_step, 1)

            def softmax_sum(it, s):
                n = it * UNITS + s
                dve.wait_ge(exp_done, n + 1)
                v = pr[:, s % 2].rearrange("p h (w k) -> p (h w) k", k=2 * WIN)
                nc.vector.tensor_reduce(ssum[:, s % 2, :], v, AX_X, ALU.add).then_inc(sum_step, 1)
                dve.wait_ge(sum_step, n * 2 + 1)
                nc.vector.reciprocal(sinv[:, s % 2, :], ssum[:, s % 2, :]).then_inc(sum_step, 1)

            def attention_sum(it, b):
                l, i = (it - 1) // NT, (it - 1) % NT
                job = ("wo", -1, b)
                slot = slot_of(job)
                if b == 0:
                    dve.wait_ge(x1_step, (it - 1) * 2 + 2)
                wait_full(dve, it, job)
                old = (l % 2) * (BATCH * ROW) + b * ROW + PAD + i * TILE
                src = ring[slot][:, 0, 0:TILE].rearrange("p (a m t) -> p m a t", a=2, m=4)
                nc.vector.tensor_tensor(x1[:, b, 1:].rearrange("p (m a t) -> p m a t", a=2, m=4), src,
                                        xt[:, bass.ds(old, TILE)].rearrange("p (m a t) -> p m a t", a=2, m=4),
                                        ALU.add).then_inc(free[slot], 1)

            def shift_x1(it):
                wait_taken(dve, it, ("wo", -1, 0))
                wait_taken(dve, it, ("wo", -1, 1))
                for lower in range(2):
                    r = slice(64 * lower, 64 * lower + 64)
                    nc.vector.tensor_copy(xf[r], x1[r, :, 1 - lower:1 - lower + TILE]).then_inc(ff_dve, 1)

            def take_mean(it):
                dve.wait_ge(ff_dve, (it - 1) * 4 + 2)
                wait_full(dve, it, ("mean", -1))
                slot = slot_of(("mean", -1))
                nc.vector.tensor_tensor(xf[:].rearrange("p b t -> p (b t)"), xf[:].rearrange("p b t -> p (b t)"),
                                        ring[slot][:, 0, :], ALU.subtract).then_inc(free[slot], 1)

            def normed(it):
                wait_taken(dve, it, ("mean", -1))
                dve.wait_ge(ff_act, (it - 1) * 2 + 2)
                wait_alone(dve, wf_in, 48 * ((it - 1) // NT) + 48, spare["dve"])
                nc.vector.scalar_tensor_tensor(out=xsq[:], in0=xf[:].rearrange("p b t -> p (b t)"), scalar=par[:, LG:LG + 1],
                                               in1=rstd[:], op0=ALU.mult, op1=ALU.mult).then_inc(ff_dve, 1)
                dve.wait_ge(ff_dve, (it - 1) * 4 + 3)
                nc.vector.tensor_scalar(xn[:], xsq[:], par[:, LB:LB + 1], None, ALU.add).then_inc(ff_dve, 1)

            def through_gate(it, c):
                m = P if c < 2 else FFR
                wait_full(dve, it, ("hidden", -1, c))
                dve.wait_ge(gated, (it - 1) * 3 + c + 1)
                slot = slot_of(("hidden", -1, c))
                nc.vector.scalar_tensor_tensor(out=gate[0:m, c, :], in0=ring[slot][0:m, 0, :], scalar=par[0:m, B1A + c:B1A + c + 1],
                                               in1=gate[0:m, c, :], op0=ALU.add, op1=ALU.mult).then_inc(free[slot], 1)

            def layer_out(it):
                l, i = (it - 1) // NT, (it - 1) % NT
                wait_full(dve, it, ("out", -1))
                slot = slot_of(("out", -1))
                for b in range(BATCH):
                    new = ((l + 1) % 2) * (BATCH * ROW) + b * ROW + PAD + i * TILE
                    last = nc.vector.scalar_tensor_tensor(out=xt[:, bass.ds(new, TILE)], in0=ring[slot][:, 0, TILE * b:TILE * (b + 1)],
                                                          scalar=par[:, B2:B2 + 1], in1=x1[:, b, 1:], op0=ALU.add, op1=ALU.add)
                last.then_inc(free[slot], 1)

            def body(it):
                wait_turns(dve, it)
                if has_old(it):
                    token_before(it)
                if has_new(it):
                    dve.wait_ge(wqk_in, 32 * (it // NT) + 32)
                    dve.wait_ge(tab_in, 16 * it + 16)
                for s in range(UNITS):
                    if has_new(it):
                        rotate(it, s, 0)
                        if s == 0:
                            set_flag(it)
                        rotate(it, s, 1)
                    if s == 3 and has_old(it):
                        normed(it)
                    if has(it, s - 1):
                        read_norms(it, s - 1)
                    if s == 2 and has_old(it):
                        take_mean(it)
                    if has(it, s - 2):
                        softmax_sum(it, s - 2)
                    if has_new(it):
                        rotate(it, s, 2)
                    if has(it, s - 1):
                        softmax_top(it, s - 1)
                    if s == 3 and has_old(it):
                        through_gate(it, 0)
                        through_gate(it, 1)
                    if has_new(it):
                        rotate(it, s, 3)
                    if s == 1 and has_new(it):
                        shift_in(it, 1)
                    if s == 1 and has_old(it):
                        for b in range(BATCH):
                            attention_sum(it, b)
                        shift_x1(it)
                    if s == 3 and has_old(it):
                        through_gate(it, 2)
                    if s == 3 and has_new(it):
                        shift_in(it + 1, 0)
                    if s == 3 and has_old(it):
                        layer_out(it)

            dve.wait_ge(consts, 16 * NCONST)
            dve.wait_ge(cleared, 5)
            shift_in(0, 0)
            body(0)
            with dve.Fori(1, TURNS) as it:
                body(it)
            body(TURNS)


def phase_join(nc, xt, x, s_dram, identity, out):
    with ExitStack() as ctx:
        def sb(name, shape, dt=F32):
            return ctx.enter_context(nc.sbuf_tensor(name, shape, dt))

        def sem(name):
            return ctx.enter_context(nc.semaphore(name))

        ident = sb("j_ident", [P, P])
        xs = sb("j_x", [P, NTOK, DIM])
        ss = sb("j_s", [P, TOKENS])
        sil = sb("j_silu", [P, 2, 512])
        prod = sb("j_prod", [P, 2, 512])
        res = sb("j_res", [P, NTOK, DIM])
        ps = [ctx.enter_context(nc.psum_tensor(f"j_ps{i}", [P, 512], F32)) for i in range(2)]
        loaded, x_loaded, silued, multiplied = sem("j_loaded"), sem("j_x_loaded"), sem("j_silued"), sem("j_multiplied")
        turned, summed, stored = sem("j_turned"), sem("j_summed"), sem("j_stored")
        groups = TOKENS // 512
        block = ctx.enter_context(nc.Block())

        def add(dve, g):
            dve.wait_ge(turned, g + 1)
            nc.vector.tensor_tensor(res[:, 4 * g:4 * g + 4, :], ps[g % 2][:].rearrange("p (n d) -> p n d", d=DIM),
                                    xs[:, 4 * g:4 * g + 4, :], ALU.add).then_inc(summed, 1)

        @block.sync
        def _(sp):
            sp.dma_start(ident[:], identity).then_inc(loaded, 16)
            sp.dma_start(ss[:], s_dram).then_inc(loaded, 16)
            sp.dma_start(xs[:], x.rearrange("b (n p) d -> p (b n) d", p=P)).then_inc(x_loaded, 16)
            o = out.rearrange("b (n p) d -> p (b n) d", p=P)
            for g in range(groups):
                sp.wait_ge(summed, g + 1)
                sp.dma_start(o[:, 4 * g:4 * g + 4, :], res[:, 4 * g:4 * g + 4, :]).then_inc(stored, 16)
            sp.wait_ge(stored, 16 * groups)

        @block.scalar
        def _(act):
            for g in range(groups):
                b, c = divmod(g, SEQ // 512)
                at = b * ROW + PAD + 512 * c
                if g >= 2:
                    act.wait_ge(multiplied, g - 1)
                nc.scalar.activation(sil[:, g % 2, :], xt[:, at:at + 512], ACT.Silu).then_inc(silued, 1)

        @block.vector
        def _(dve):
            dve.wait_ge(loaded, 32)
            dve.wait_ge(x_loaded, 16)
            for g in range(groups):
                dve.wait_ge(silued, g + 1)
                if g >= 2:
                    dve.wait_ge(turned, g - 1)
                nc.vector.tensor_tensor(prod[:, g % 2, :], sil[:, g % 2, :], ss[:, 512 * g:512 * (g + 1)],
                                        ALU.mult).then_inc(multiplied, 1)
                if g >= 1:
                    add(dve, g - 1)
            add(dve, groups - 1)

        @block.tensor
        def _(pe):
            pe.wait_ge(loaded, 32)
            for g in range(groups):
                pe.wait_ge(multiplied, g + 1)
                if g >= 2:
                    pe.wait_ge(summed, g - 1)
                for k in range(4):
                    last = nc.tensor.transpose(ps[g % 2][:, P * k:P * (k + 1)], prod[:, g % 2, P * k:P * (k + 1)], ident[:])
                last.then_inc(turned, 1)


def build(nc, d, s_dram, out):
    with nc.sbuf_tensor("xt", [P, 2 * BATCH * ROW], F32) as xt:
        phase_norm(nc, d["x"], xt, d["identity"])
        phase_mamba(nc, xt, d, s_dram)
        phase_layers(nc, xt, d)
        phase_join(nc, xt, d["x"], s_dram, d["identity"], out)


def shape_constants():
    f32 = np.float32
    half = np.arange(0, DH, 2, dtype=f32)
    inv_freq = f32(1.0) / f32(10000.0) ** (half / f32(DH))
    t = np.arange(SEQ, dtype=f32)
    freqs = t[:, None] * inv_freq[None, :]
    base = (half + f32(0.4 * DH)) / f32(1.4 * DH)
    power = (t - SEQ // 2) / f32(WIN // 2)
    scale = base[None, :] ** power[:, None]
    rows = np.arange(P) % 32
    sign = np.where(np.arange(P) % DH < DH // 2, -1.0, 1.0).astype(f32)[:, None]
    cos, sin, sc = np.cos(freqs).T[rows], np.sin(freqs).T[rows] * sign, scale.T[rows]
    tables = np.stack([cos * sc, sin * sc, cos * (f32(1.0) / sc), sin * (f32(1.0) / sc)], 1).astype(f32)
    tables = tables.reshape(P, 4, NT, TILE).transpose(0, 2, 1, 3).reshape(P, -1)
    flags = np.where(np.arange(NT) > 0, 1.0, 0.0).astype(f32)[None, :].repeat(P, 0)
    q = (np.arange(P) % WIN)[:, None]
    key = np.arange(2 * WIN)[None, :]
    seen = np.where(key < WIN, key >= q, key - WIN <= q)
    one = np.where(seen, 0.0, MASKED)
    first = np.where(seen & (key >= WIN), 0.0, MASKED)
    bf16 = np.dtype("bfloat16")
    pick = np.zeros((2, 32, 32, P), f32)
    pick[:, np.arange(32), np.arange(32), :] = 1.0
    ones_half = np.zeros((P, 2, WIN), f32)
    ones_half[:64, 0], ones_half[64:, 1] = 1.0, 1.0
    halves = np.zeros((P, 2), f32)
    halves[:64, 0], halves[64:, 1] = 1.0, 1.0
    small = np.ones((P, 2), f32)
    small[:, 0], small[:, 1] = EPS, LN_SHIFT / 2 * np.log(2.0)
    return {
        "tables": tables, "flags": flags, "mask": np.tile(one, (1, NWIN)).astype(bf16),
        "mask0": np.concatenate([first] + [one] * (NT - 1), 1).astype(bf16),
        "identity": np.eye(P, dtype=f32), "identity_b": np.eye(P).astype(bf16), "pick": pick.reshape(64, 32, P),
        "ones_half": ones_half, "halves": halves, "mean_w": np.full((P, P), 1.0 / DIM, f32), "small": small,
    }


def laid_out(a):
    def cols(v, n):
        return v.reshape(n, P).T

    f32 = np.float32
    w_x = a["L0_attn_x_proj_w"].T
    w_x = np.concatenate([w_x, w_x[:, DT_RANK:]], 1)
    swap = np.arange(DH).reshape(2, DH // 2)[::-1].reshape(-1)
    wqkv = a["L0_ffn_Wqkv"].astype(f32)
    qk = wqkv[:, :, :2 * INNER].reshape(DEPTH, DIM, 2, 8, 2, DH)
    qk = np.stack([qk, qk[..., swap]], 4).reshape(DEPTH, DIM, -1)
    vec = np.zeros((P, 32), f32)
    vec[:, 0:4] = cols(a["L0_attn_in_proj_b"], 4)
    vec[:, 4:6] = cols(a["L0_attn_conv_b"], 2)
    vec[:, 6:8] = cols(a["L0_attn_dt_proj_b"], 2)
    vec[:, 8:10] = cols(a["L0_attn_D_param"], 2)
    vec[:, 10] = a["L0_attn_out_proj_b"]
    vec[:, 12:20] = a["L0_attn_conv_w"].reshape(2, P, CONV).transpose(1, 0, 2).reshape(P, -1)
    parq = np.zeros((P, DEPTH, NPARQ), f32)
    par = np.zeros((P, DEPTH, NPAR - NPARQ), f32)
    for k, name in enumerate(("L0_ffn_q_scale", "L0_ffn_k_scale")):
        v = a[name].T
        parq[:, :, 2 * k] = np.tile(v, (2, 1))
        parq[:, :, 2 * k + 1] = np.tile(v[swap], (2, 1))
    par[:, :, LG], par[:, :, LB], par[:, :, B2] = a["L0_ffn_ln_g"].T, a["L0_ffn_ln_b"].T, a["L0_ffn_b2"].T
    for part, at in ((0, B1A), (1, B1G)):
        for c in range(3):
            m = P if c < 2 else FFR
            par[:m, :, at + c] = a["L0_ffn_b1"][:, FF * part + P * c:FF * part + P * c + m].T
    w2 = np.zeros((DEPTH, 3 * P, DIM), f32)
    w2[:, :FF] = a["L0_ffn_W2"]
    return {
        "x": a["L0_attn_hidden_states"],
        "w_in": a["L0_attn_in_proj_w"].T,
        "w_x": w_x.reshape(2, P, -1).transpose(1, 0, 2),
        "w_dt": a["L0_attn_dt_proj_w"].T,
        "w_out": a["L0_attn_out_proj_w"].T.reshape(2, P, DIM).transpose(1, 0, 2),
        "m_vec": vec,
        "alog": a["L0_attn_A_log"].reshape(2, P, STATE).transpose(1, 0, 2),
        "wqk": qk.transpose(1, 0, 2).reshape(P, -1),
        "wv": wqkv[:, :, 2 * INNER:].transpose(1, 0, 2).reshape(P, -1),
        "wo": a["L0_ffn_Wo"].reshape(DEPTH, 8, P, DIM).transpose(2, 0, 1, 3).reshape(P, -1),
        "w1": a["L0_ffn_W1"].transpose(1, 0, 2).reshape(P, -1),
        "w2": w2.reshape(DEPTH, 3, P, DIM).transpose(2, 0, 1, 3).reshape(P, -1),
        "parq": parq.reshape(P, -1),
        "par": par.reshape(P, -1),
    }


def kernel(**inputs):
    from concourse import bacc
    from concourse.bass_utils import run_bass_kernel_spmd

    nc = bacc.Bacc("TRN2", target_bir_lowering=False, num_devices=1)
    arrays = {k: np.ascontiguousarray(v) for k, v in
              {**laid_out({k: np.asarray(v) for k, v in inputs.items()}), **shape_constants()}.items()}
    d = {k: nc.dram_tensor(f"in_{k}", v.shape, mybir.dt.from_np(v.dtype), kind="ExternalInput").ap() for k, v in arrays.items()}
    s_dram = nc.dram_tensor("mamba_out", (P, TOKENS), F32, kind="Internal").ap()
    out = nc.dram_tensor("out", (BATCH, SEQ, DIM), F32, kind="ExternalOutput").ap()
    build(nc, d, s_dram, out)
    r = run_bass_kernel_spmd(nc, [{f"in_{k}": v for k, v in arrays.items()}], core_ids=[0])
    return r.results[0]["out"]
```
